# Optimizing a Trainium2 kernel written in Bass

```python
import numpy as np
import jax
import jax.numpy as jnp

def _softmax(x, axis=-1):
    return jax.nn.softmax(x, axis=axis)

def _gelu(x):
    return jax.nn.gelu(x, approximate=True)

def _silu(x):
    return jax.nn.silu(x)

def _sigmoid(x):
    return jax.nn.sigmoid(x)

def _layernorm(x, axis=-1, eps=1e-05):
    m = jnp.mean(x, axis=axis, keepdims=True)
    v = jnp.var(x, axis=axis, keepdims=True)
    return (x - m) / jnp.sqrt(v + eps)

def _scatter_add(tgt, idx, src, axis=0):
    return tgt.at[idx].add(src)

def _segment_sum(src, seg, n):
    return jax.ops.segment_sum(src, seg, n)
kernel_name = 'mk_decoder_preln_d1_seqx_r8_847838'

def setup_inputs(seed: int=0):
    np.random.seed(seed)
    _w = jnp.asarray

    def _rec_inputs():
        import jax
        import jax.numpy as jnp
        _rk = jax.random.key(seed)
        x = -0.0003929 + 0.9999 * jax.random.normal(jax.random.fold_in(_rk, 1), (32, 56, 128), jnp.float32)
        _lenS = 56 - jax.random.randint(jax.random.fold_in(_rk, 7), (32,), 0, max(1, 56 // 4) + 1, jnp.int32)
        _lenS2 = 1500 - jax.random.randint(jax.random.fold_in(_rk, 8), (32,), 0, max(1, 1500 // 4) + 1, jnp.int32)
        _ctx_1024P = jax.random.normal(jax.random.fold_in(_rk, 11), (32, 16, 128), jnp.float32)
        _ctx_1024c = jax.random.dirichlet(jax.random.fold_in(_rk, 511), 0.3 * jnp.ones((16,), jnp.float32), (32, 1500))
        _ctx_1024t = jnp.einsum('bsk,bkd->bsd', _ctx_1024c, _ctx_1024P)
        _ctx_1024t = _ctx_1024t * jax.lax.rsqrt(jnp.mean(jnp.square(_ctx_1024t)) + 1e-12) * 0.953939
        ctx_1024 = 2.81802e-05 + 1.00001 * (_ctx_1024t + 0.3 * jax.random.normal(jax.random.fold_in(_rk, 611), (32, 1500, 128), jnp.float32))
        return (x, ctx_1024)
    x, ctx_1024 = _rec_inputs()

    def _L0_attn_setup():
        import jax, jax.numpy as jnp
        import numpy as np
        NHEAD = 16

        def _rope_cos_sin(T, D, dtype):
            inv_freq = 1.0 / 10000.0 ** (jnp.arange(0, D, 2, dtype=jnp.float32) / D)
            freqs = jnp.arange(T, dtype=jnp.float32)[:, None] * inv_freq[None, :]
            return (jnp.cos(freqs).astype(dtype), jnp.sin(freqs).astype(dtype))

        def _apply_rope(x, cos, sin):
            x1, x2 = (x[..., ::2], x[..., 1::2])
            return jnp.concatenate([x1 * cos - x2 * sin, x1 * sin + x2 * cos], axis=-1)
        key = jax.random.key(seed)
        k1, k2, k3, k4 = jax.random.split(key, 4)
        B, T, C = (2, 256, 128)
        s = 1.0 / np.sqrt(C)
        x = jax.random.normal(k1, (B, T, C), jnp.float32)
        w_qkv = jax.random.normal(k2, (3 * C, C), jnp.float32) * s
        w_proj = jax.random.normal(k3, (C, C), jnp.float32) * s
        b_proj = jax.random.normal(k4, (C,), jnp.float32) * 0.01
        return {'x': x, 'w_qkv': w_qkv, 'w_proj': w_proj, 'b_proj': b_proj}
    _L0_attn_all = _L0_attn_setup()
    _L0_attn_in = {k: v for k, v in _L0_attn_all.items() if k in ('w_qkv', 'w_proj', 'b_proj')}
    del _L0_attn_all

    def _L0_xattn_setup():
        import jax, jax.numpy as jnp
        import numpy as np
        DIM = 128
        V_DIM = 128
        NUM_HEADS = 8
        SCALE = (DIM // NUM_HEADS) ** (-0.5)
        key = jax.random.key(seed)
        ks = jax.random.split(key, 8)
        B, N, M = (4, 512, 512)
        s = 0.02
        return {'xq': jax.random.normal(ks[0], (B, N, DIM), jnp.float32), 'xk': jax.random.normal(ks[1], (B, M, DIM), jnp.float32), 'xv': jax.random.normal(ks[2], (B, M, V_DIM), jnp.float32), 'wq': jax.random.normal(ks[3], (DIM, DIM), jnp.float32) * s, 'wk': jax.random.normal(ks[4], (DIM, DIM), jnp.float32) * s, 'wv': jax.random.normal(ks[5], (V_DIM, V_DIM), jnp.float32) * s, 'w_proj': jax.random.normal(ks[6], (V_DIM, DIM), jnp.float32) * s, 'b_proj': jax.random.normal(ks[7], (DIM,), jnp.float32) * s}
    _L0_xattn_all = _L0_xattn_setup()
    _L0_xattn_in = {k: v for k, v in _L0_xattn_all.items() if k in ('wq', 'wk', 'wv', 'w_proj', 'b_proj')}
    del _L0_xattn_all

    def _L0_ffn_setup():
        import jax, jax.numpy as jnp
        import numpy as np
        B, S, H = (2, 128, 128)
        KD, NH, K = (128, 8, 8)
        NE = 8192
        NK = 32
        EPS = 1e-05
        key = jax.random.key(seed)
        ks = jax.random.split(key, 5)
        inputs = jax.random.normal(ks[0], (B, S, H), jnp.float32)
        bn_gamma = jnp.ones((H,), jnp.float32)
        bn_beta = jnp.zeros((H,), jnp.float32)
        w_q = jax.random.normal(ks[1], (2 * NH * KD, H), jnp.float32) * (1.0 / np.sqrt(H))
        keys_p = jax.random.normal(ks[2], (NH, NK, 2, KD), jnp.float32) * 0.02
        lim = float(np.sqrt(6.0 / (NE + H)))
        down = jax.random.uniform(ks[3], (NE, H), jnp.float32, -lim, lim)
        up = jax.random.uniform(ks[4], (NE, H), jnp.float32, -lim, lim)
        return {'inputs': inputs, 'bn_gamma': bn_gamma, 'bn_beta': bn_beta, 'w_q': w_q, 'keys_p': keys_p, 'down': down, 'up': up}
    _L0_ffn_all = _L0_ffn_setup()
    _L0_ffn_in = {k: v for k, v in _L0_ffn_all.items() if k in ('bn_gamma', 'bn_beta', 'w_q', 'keys_p', 'down', 'up')}
    del _L0_ffn_all
    return {'x': x, 'ctx_1024': ctx_1024, 'L0_attn_w_qkv': _L0_attn_in['w_qkv'], 'L0_attn_w_proj': _L0_attn_in['w_proj'], 'L0_attn_b_proj': _L0_attn_in['b_proj'], 'L0_xattn_wq': _L0_xattn_in['wq'], 'L0_xattn_wk': _L0_xattn_in['wk'], 'L0_xattn_wv': _L0_xattn_in['wv'], 'L0_xattn_w_proj': _L0_xattn_in['w_proj'], 'L0_xattn_b_proj': _L0_xattn_in['b_proj'], 'L0_ffn_bn_gamma': _L0_ffn_in['bn_gamma'], 'L0_ffn_bn_beta': _L0_ffn_in['bn_beta'], 'L0_ffn_w_q': _L0_ffn_in['w_q'], 'L0_ffn_keys_p': _L0_ffn_in['keys_p'], 'L0_ffn_down': _L0_ffn_in['down'], 'L0_ffn_up': _L0_ffn_in['up']}

def reference(x, ctx_1024, L0_attn_w_qkv, L0_attn_w_proj, L0_attn_b_proj, L0_xattn_wq, L0_xattn_wk, L0_xattn_wv, L0_xattn_w_proj, L0_xattn_b_proj, L0_ffn_bn_gamma, L0_ffn_bn_beta, L0_ffn_w_q, L0_ffn_keys_p, L0_ffn_down, L0_ffn_up):
    import jax
    import jax.numpy as jnp

    def _L0_attn_ref(x, w_qkv, w_proj, b_proj):
        import jax, jax.numpy as jnp
        import numpy as np
        NHEAD = 16

        def _rope_cos_sin(T, D, dtype):
            inv_freq = 1.0 / 10000.0 ** (jnp.arange(0, D, 2, dtype=jnp.float32) / D)
            freqs = jnp.arange(T, dtype=jnp.float32)[:, None] * inv_freq[None, :]
            return (jnp.cos(freqs).astype(dtype), jnp.sin(freqs).astype(dtype))

        def _apply_rope(x, cos, sin):
            x1, x2 = (x[..., ::2], x[..., 1::2])
            return jnp.concatenate([x1 * cos - x2 * sin, x1 * sin + x2 * cos], axis=-1)
        B, T, C = x.shape
        H = NHEAD
        D = C // H
        scale = D ** (-0.5)
        qkv = (x @ w_qkv.T).reshape(B, T, 3, H, D).transpose(2, 0, 3, 1, 4)
        q, k, v = (qkv[0], qkv[1], qkv[2])
        cos, sin = _rope_cos_sin(T, D, x.dtype)
        q = _apply_rope(q, cos, sin)
        k = _apply_rope(k, cos, sin)
        attn = jax.nn.softmax(jnp.einsum('bhqd,bhkd->bhqk', q, k) * scale, axis=-1)
        out = jnp.einsum('bhqk,bhkd->bhqd', attn, v).transpose(0, 2, 1, 3).reshape(B, T, C)
        return out @ w_proj.T + b_proj

    def _L0_xattn_ref(xq, xk, xv, wq, wk, wv, w_proj, b_proj):
        import jax, jax.numpy as jnp
        import numpy as np
        DIM = 128
        V_DIM = 128
        NUM_HEADS = 8
        SCALE = (DIM // NUM_HEADS) ** (-0.5)
        q = jnp.einsum('bnc,cd->bnd', xq, wq)
        k = jnp.einsum('bmc,cd->bmd', xk, wk)
        v = jnp.einsum('bmc,cd->bmd', xv, wv)
        attn = jnp.einsum('bnd,bmd->bnm', q, k) * SCALE
        attn = jax.nn.softmax(attn, axis=-1)
        x = jnp.einsum('bnm,bmd->bnd', attn, v)
        x = jnp.einsum('bnd,dc->bnc', x, w_proj) + b_proj
        return x

    def _L0_ffn_ref(inputs, bn_gamma, bn_beta, w_q, keys_p, down, up):
        import jax, jax.numpy as jnp
        import numpy as np
        B, S, H = (2, 128, 128)
        KD, NH, K = (128, 8, 8)
        NE = 8192
        NK = 32
        EPS = 1e-05
        b, s, d = inputs.shape
        x = inputs.reshape(b * s, d)
        mean = x.mean(axis=0)
        var = x.var(axis=0)
        xn = (x - mean) * jax.lax.rsqrt(var + EPS) * bn_gamma + bn_beta
        xn = xn.reshape(b, s, d)
        q = (xn @ w_q.T).reshape(b, s, 2, NH, KD).transpose(2, 0, 1, 3, 4)
        sim = jnp.einsum('pbnhd,hkpd->pbnhk', q, keys_p)
        scores, idx = jax.lax.top_k(sim, K)
        all_scores = (scores[0][..., :, None] + scores[1][..., None, :]).reshape(b, s, NH, K * K)
        all_idx = (idx[0][..., :, None] * NK + idx[1][..., None, :]).reshape(b, s, NH, K * K)
        sc, pk = jax.lax.top_k(all_scores, K)
        indices = jnp.take_along_axis(all_idx, pk, axis=-1)
        wd = down[indices]
        hmid = jnp.einsum('bnd,bnhkd->bnhk', inputs, wd)
        hmid = jax.nn.sigmoid(sc) * jax.nn.gelu(hmid, approximate=False)
        wu = up[indices]
        return jnp.einsum('bnhk,bnhkd->bnd', hmid, wu)
    x = x + _L0_attn_ref(_layernorm(x, axis=-1), L0_attn_w_qkv, L0_attn_w_proj, L0_attn_b_proj)
    x = x + _L0_xattn_ref(_layernorm(x, axis=-1), ctx_1024, ctx_1024, L0_xattn_wq, L0_xattn_wk, L0_xattn_wv, L0_xattn_w_proj, L0_xattn_b_proj)
    x = x + _L0_ffn_ref(_layernorm(x, axis=-1), L0_ffn_bn_gamma, L0_ffn_bn_beta, L0_ffn_w_q, L0_ffn_keys_p, L0_ffn_down, L0_ffn_up)
    return x

_drawn_inputs = setup_inputs


def setup_inputs(seed=0):
    import zlib

    import numpy as np

    out = dict(_drawn_inputs(seed))
    spreads = {'L0_ffn_bn_gamma': (1.0, 0.6), 'L0_ffn_bn_beta': (0.0, 0.8)}
    factors = {'L0_attn_b_proj': 5.708,
     'L0_xattn_wq': 8.0,
     'L0_xattn_wk': 8.0,
     'L0_xattn_b_proj': 2.759,
     'L0_ffn_w_q': 7.344,
     'L0_ffn_keys_p': 7.285,
     'L0_ffn_down': 7.154,
     'L0_ffn_up': 7.122}
    for name, (base, spread) in spreads.items():
        noise = np.random.default_rng([zlib.crc32(name.encode()), seed]).standard_normal(out[name].shape)
        drawn = base * np.exp(spread * noise) if base else spread * noise
        out[name] = jnp.asarray(drawn.astype(out[name].dtype))
    for name, factor in factors.items():
        out[name] = (out[name] * factor).astype(out[name].dtype)
    return out
```

```python
import concourse.bass as bass
from concourse import mybir
from contextlib import ExitStack

F32 = mybir.dt.float32
F16 = mybir.dt.float16
U16 = mybir.dt.uint16
ALU = mybir.AluOpType
ACT = mybir.ActivationFunctionType
AX = mybir.AxisListType

B, T, C = 32, 56, 128
CTX = 1500
HEADS, HD = 16, 8
NH, NK, TOPK = 8, 32, 8
TP = 64
PAIRS = B // 2
CHUNK = 4
TOK = B * T
ROWS = 125
NT = CTX // ROWS
BANK = 512
TG = 4
NG = NT // TG
SPREAD = 112
RING = 4
TILE = 128
DUOS = TOK // (2 * TILE)
EXPERTS = NK * NK
U, V = 128, 8
HK = NH * TOPK
PARTS = ((0, 8), (1, 4), (2, 2), (4, 1))
NCAND = 20
LN_EPS = 1e-5
BN_EPS = 1e-5
W_UP = 16384.0

PACK_A = [("wq", C), ("wqs", C), ("wk", C), ("wks", C), ("wv", C), ("wproj", C),
          ("xwq", C), ("xwk", C), ("xwv", C), ("xproj", C), ("ident", C), ("cos", 2 * TP), ("sin", 2 * TP),
          ("slot", 4), ("group", 4), ("vmask", C), ("bias1", C), ("bias2", C), ("gamma", 1), ("beta", 1)]
PACK_B = [("keys", 2 * NH * NK), ("down", EXPERTS), ("up", EXPERTS)]


def columns(pack):
    at, out = 0, {}
    for name, n in pack:
        out[name] = (at, at + n)
        at += n
    return out, at


class Chain:

    def __init__(self, eng, sem):
        self.eng, self.sem, self.base, self.n = eng, sem, 0, 0

    def did(self, ins):
        ins.then_inc(self.sem, 1)
        self.n += 1
        return ins

    def wait(self):
        self.eng.wait_ge(self.sem, self.base + self.n)

    def wait_apart(self, stand):
        self.wait()
        self.eng.sem_inc(stand, 1)

    def enter(self, i, per_pass):
        self.start, self.per_pass = self.n, per_pass
        self.base = i * per_pass

    def leave(self, passes):
        assert self.n - self.start == self.per_pass, (self.n - self.start, self.per_pass)
        self.n, self.base = self.start + self.per_pass * passes, 0


def decoder_block(nc, x, ctx, pack_a, pack_b, pack_q, out):
    ca, na = columns(PACK_A)
    cb, nb = columns(PACK_B)
    with ExitStack() as stack:
        def sb(name, shape, dt=F32):
            return stack.enter_context(nc.sbuf_tensor(name, shape, dt))

        def sem(name):
            return stack.enter_context(nc.semaphore(name))

        KA = sb("KA", [128, na])
        KB = sb("KB", [128, nb])
        def wa(name):
            return KA[:, ca[name][0]:ca[name][1]]
        def wb(name):
            return KB[:, cb[name][0]:cb[name][1]]
        ident = wa("ident")

        XA = sb("XA", [128, 4 * PAIRS * C])
        def xpart(n):
            return XA[:, n * PAIRS * C:(n + 1) * PAIRS * C].rearrange("p (a c) -> p a c", c=C)
        x0 = xpart(0)
        x1 = xpart(1)
        xl2T = XA[:, 2 * PAIRS * C:3 * PAIRS * C]
        q2T = XA[:, 3 * PAIRS * C:4 * PAIRS * C]
        iota_u = XA[:, :].bitcast(U16).rearrange("p (u n) -> p u n", u=U)
        xn_ = sb("xn", [128, PAIRS, C])
        x2 = sb("x2", [128, PAIRS, C])
        x2T = sb("x2T", [128, TOK])
        xlT = sb("xlT", [128, TOK])
        stats = sb("stats", [128, PAIRS, 6])
        mv = sb("mv", [128, PAIRS, 2])
        rstd = sb("rstd", [128, PAIRS])
        veps = sb("veps", [128, PAIRS])
        A2 = sb("A2", [128, C])
        Wvp = sb("Wvp", [128, C])
        Wsim = sb("Wsim", [128, 2 * NH * NK])

        CTXF = 2 * NT * C
        ARENA = RING * CTXF + 2 * CTXF + 2 * CTX + NT * 128 + 1536
        AR = sb("AR", [128, ARENA])
        used = [0]
        def take(n):
            at = used[0]
            used[0] += n
            assert used[0] <= ARENA, (used[0], ARENA)
            return AR[:, at:at + n]
        ring = [take(CTXF).rearrange("p (b t c) -> p b t c", b=2, t=NT) for _ in range(RING)]
        after_ring = used[0]
        ctxT = [take(2 * CTX).rearrange("p (b g m) -> p b g m", b=2, g=NG) for _ in range(2)]
        prob2 = [take(CTX) for _ in range(2)]
        prob2T = take(NT * 128).rearrange("p (t n) -> p t n", t=NT)
        q2 = [take(128) for _ in range(2)]
        oT = take(128)
        used[0] = after_ring
        TC = CHUNK * 128
        xc = take(TC).rearrange("p (a c) -> p a c", c=C)
        xcT = take(TC)
        xcT2 = take(2 * TC).rearrange("p (b r n) -> p b r n", b=2 * CHUNK, r=2)
        rope_c = take(TC)
        rope_s = take(TC)
        rot = take(TC)
        qx = take(4 * TC).rearrange("p (g n) -> p g n", g=4)
        kx = take(4 * TC).rearrange("p (g n) -> p g n", g=4)
        fwq = kx.rearrange("p g n -> p (g n)")
        prob1 = [take(HEADS * TP).rearrange("p (h k) -> p h k", h=HEADS) for _ in range(2)]
        prob1T = take(HEADS // 2 * 128).rearrange("p (h n) -> p h n", n=128)
        vx = take(2 * C).rearrange("p (b h d) -> p b h d", b=2, d=2 * HD)
        att = take(C)
        attT = take(C)
        used[0] = 0
        gelu = take(V * TOK).rearrange("p (v n) -> p v n", v=V)
        pick_u = take(U * TILE // 2).bitcast(F16).rearrange("p (u n) -> p u n", u=U)
        neg1 = sb("neg1", [128, HEADS])
        sum1 = sb("sum1", [128, HEADS])
        inv1 = sb("inv1", [128, HEADS])
        max2 = sb("max2", [128, 1])
        nb2 = sb("nb2", [128, 1])
        sum2 = sb("sum2", [128, 2])
        inv2 = sb("inv2", [128, 2])
        bst = sb("bst", [128, 4, 6])
        bmv = sb("bmv", [128, 2])
        bsc = sb("bsc", [128, 4])
        xbn = sb("xbn", [128, 2, TILE])
        x2s = sb("x2s", [128, 2, TILE])
        val = sb("val", [128, 2, 2, NH, TOPK])
        idx = sb("idx", [128, 2, 2, NH, TOPK], U16)
        idf = sb("idf", [128, 2, 2, NH, TOPK])
        cand = sb("cand", [128, 2, NH, NCAND])
        cexp = sb("cexp", [128, 2, NH, NCAND])
        best = sb("best", [128, 2, NH, TOPK])
        pos = sb("pos", [128, 2, NH, TOPK], U16)
        hit = sb("hit", [128, NH, NCAND, TOPK], F16)
        hite = xn_[:, :, :].rearrange("p a c -> p (a c)")[:, 0:NH * NCAND * TOPK].rearrange("p (h c k) -> p h c k", h=NH, c=NCAND)
        expert = sb("expert", [128, 2, HK])
        weight = sb("weight", [128, 2, HK])
        eT = sb("eT", [128, TILE], U16)
        eu = sb("eu", [128, TILE], U16)
        ev = sb("ev", [128, TILE], U16)
        w_hi = sb("w_hi", [128, TILE], F16)
        w_lo = sb("w_lo", [128, TILE], F16)
        pick_v = sb("pick_v", [128, V, TILE], F16)
        b_hi = sb("b_hi", [128, 2 * V, TILE], F16)
        b_lo = sb("b_lo", [128, 2 * V, TILE], F16)
        act_w = x2[:, :, :].rearrange("p a c -> p (a c)").rearrange("p (t v n) -> p t v n", t=2, v=V)
        iota_v = sb("iota_v", [128, V, TILE], U16)
        iota_c = sb("iota_c", [128, NCAND, TOPK], U16)
        res = sb("res", [128, 2, C])

        PS = stack.enter_context(nc.psum_tensor("PS", [128, 8, BANK], F32))
        def bank(n, a=0, b=BANK):
            return PS[:, n, a:b]

        s = {n: sem(n) for n in (
            "x_in ka_in kb_in out_done ctx0 ctx1 ctx2 ctx3 "
            "dve act pool apart apart_pool pads_zero ones_done folded fold_copied bias_added "
            "ln1_var ln1_std ln1_done xc_ready xcT_psum xcT_ready xcT2_ready qk_psum rope_read rot_ready expanded "
            "s1_psum s1_read v_psum v_ready p1_ready p1T_psum p1T_a p1T_b o1_psum att_ready attT_psum attT_ready "
            "y1_psum x1_done "
            "ln_var ln_std ln_done t_psum t_copied q2_psum q2_copied q2_ready "
            "cT_psum0 cT_psum1 cT_a cT_d s2_psum m2_ready p2_ready p2T_psum p2T_a p2T_d o2_psum oT_ready y2_psum x2_done "
            "bn_var bn_std bn_ready h_psum h_done iota_done "
            "xbn_ready sim_psum sim_read best_ready weight_ready cexp_ready hit_ready hite_ready expert_ready "
            "x2s_ready ew_psum picks mix_psum mixed out_psum res_ready").split()}
        block = stack.enter_context(nc.Block())

        @block.sync
        def _(sp):
            sp.sem_inc(s["out_done"], 16)
            rows_out = out.rearrange("b t c -> (b t) c")
            sp.dma_start(KA[:, :], pack_a).then_inc(s["ka_in"], 16)
            for b in range(2):
                sp.wait_ge(s["pads_zero"], 1)
                sp.dma_start(x0[b * TP:b * TP + T, :, :],
                             x.rearrange("(a b) t c -> b t a c", b=2)[b]).then_inc(s["x_in"], 16)
            sp.dma_start(KB[:, :], pack_b).then_inc(s["kb_in"], 16)
            sp.dma_start(fwq, pack_q).then_inc(s["kb_in"], 16)

            def load(p, slot):
                src = ctx[bass.ds(2 * p, 2), :, :].rearrange("b (p t) c -> p b t c", t=NT)
                for a, z in ((0, SPREAD), (SPREAD, ROWS)):
                    sp.dma_start(ring[slot][a:z], src[a:z]).then_inc(s[f"ctx{slot}"], 16)

            for p in range(RING):
                load(p, p)
            with sp.Fori(0, PAIRS // RING - 1) as i:
                for j in range(RING):
                    sp.wait_ge(s["o2_psum"], i * RING + (j + 1))
                    load((i + 1) * RING + j, j)
            with sp.Fori(0, DUOS) as i:
                sp.wait_ge(s["res_ready"], i + 2)
                sp.dma_start(rows_out[bass.ds(i * 2 * TILE, 2 * TILE), :].rearrange("(t p) c -> p t c", p=TILE),
                             res[:, :, :]).then_inc(s["out_done"], 16)
            sp.wait_ge(s["out_done"], 16 * DUOS + 16)

        @block.gpsimd
        def _(pool):
            ch = Chain(pool, s["pool"])
            ch.did(nc.gpsimd.memset(x0[32:64, :, :], 0.0))
            ch.wait()
            ch.did(nc.gpsimd.memset(x0[96:128, :, :], 0.0))
            ch.wait()
            pool.sem_inc(s["pads_zero"], 1)
            for n in range(2):
                ch.did(nc.gpsimd.memset(prob1[n], 0.0))
            ch.did(nc.gpsimd.memset(b_hi[:, :, :], 0.0))
            ch.did(nc.gpsimd.memset(b_lo[:, :, :], 0.0))
            ch.did(nc.gpsimd.iota(iota_v[:, :, :], pattern=[[1, V], [0, TILE]], base=0, channel_multiplier=0))
            ch.did(nc.gpsimd.iota(iota_c[:, :, :], pattern=[[1, NCAND], [0, TOPK]], base=0, channel_multiplier=0))
            ch.wait()
            pool.sem_inc(s["ones_done"], 1)
            with pool.Fori(0, PAIRS // CHUNK) as c:
                pool.wait_ge(s["ln1_done"], 1)
                pool.wait_ge(s["xcT_ready"], c + 1)
                pool.sem_inc(s["apart_pool"], 1)
                nc.gpsimd.tensor_copy(xc, xn_[:, bass.ds(c * CHUNK, CHUNK), :]).then_inc(s["xc_ready"], 1)
                pool.wait_ge(s["xcT_ready"], c + 2)
                pool.sem_inc(s["apart_pool"], 1)
                nc.gpsimd.tensor_copy(xcT2, xcT.rearrange("p (b o n) -> p b o n", b=2 * CHUNK, o=1).to_broadcast([128, 2 * CHUNK, 2, TP])).then_inc(s["xcT2_ready"], 1)
            pool.wait_ge(s["q2_copied"], 4)
            for p in range(2):
                nc.gpsimd.tensor_copy(q2[p], q2T[:, p * 128:(p + 1) * 128]).then_inc(s["q2_ready"], 1)
            with pool.Fori(0, PAIRS // 2 - 1) as i:
                for j in range(2):
                    pool.wait_ge(s["s2_psum"], 2 * i + (j + 1))
                    pool.sem_inc(s["apart_pool"], 1)
                    nc.gpsimd.tensor_copy(q2[j], q2T[:, bass.ds((2 * i + 2 + j) * 128, 128)]).then_inc(s["q2_ready"], 1)
            def residual(i):
                for t in range(2):
                    last = nc.gpsimd.tensor_copy(x2s[:, t, :], x2T[:, bass.ds(i * 2 * TILE + t * TILE, TILE)])
                last.then_inc(s["x2s_ready"], 1)
            pool.wait_ge(s["x2_done"], PAIRS + 1)
            nc.gpsimd.iota(iota_u, pattern=[[V, U], [0, TILE]], base=0, channel_multiplier=0).then_inc(s["iota_done"], 1)
            pool.wait_ge(s["t_copied"], 12)
            residual(0)
            with pool.Fori(0, DUOS - 1) as i:
                pool.wait_ge(s["out_psum"], i + 1)
                pool.sem_inc(s["apart_pool"], 1)
                residual(i + 1)

        def self_attention_act(act, c):
            act.wait_ge(s["xcT_psum"], c + 1)
            nc.scalar.activation(xcT, bank(6), ACT.Copy).then_inc(s["xcT_ready"], 1)
            for n, dst in enumerate((qx, kx)):
                act.wait_ge(s["rot_ready"], 2 * c + (n + 1))
                for g in range(4):
                    k0 = ca["group" if n == 0 else "slot"][0]
                    last = nc.scalar.activation(dst[:, g, :], rot, ACT.Copy, scale=KA[:, k0 + g:k0 + g + 1])
                last.then_inc(s["expanded"], 1)

            def softmax(j):
                act.wait_ge(s["s1_read"], c * CHUNK + (j + 1))
                nc.scalar.activation(prob1[j % 2][:, :, 0:T], prob1[j % 2][:, :, 0:T], ACT.Exp, scale=HD ** -0.5).then_inc(s["p1_ready"], 1)

            def rest(j):
                act.wait_ge(s["p1T_psum"], 2 * (c * CHUNK) + 2 * j + 1)
                nc.scalar.activation(prob1T[:, 0:4, :], bank(4).rearrange("p (h n) -> p h n", h=4), ACT.Copy).then_inc(s["p1T_a"], 1)
                act.wait_ge(s["attT_psum"], c * CHUNK + (j + 1))
                nc.scalar.activation(attT, bank(7, 384, 512), ACT.Copy).then_inc(s["attT_ready"], 1)

            for j in range(CHUNK):
                softmax(j)
                if j:
                    rest(j - 1)
            rest(CHUNK - 1)

        @block.scalar
        def _(act):
            for n, dst in enumerate((A2, Wvp)):
                act.wait_ge(s["folded"], n + 1)
                nc.scalar.activation(dst[:, :], bank(7 - n, 0, 128), ACT.Copy).then_inc(s["fold_copied"], 1)
            act.wait_ge(s["folded"], 3)
            nc.scalar.activation(Wsim[:, :], bank(5), ACT.Copy).then_inc(s["fold_copied"], 1)
            act.wait_ge(s["ln1_var"], 1)
            nc.scalar.activation(rstd[:, :], veps[:, :], ACT.Sqrt).then_inc(s["ln1_std"], 1)
            act.wait_ge(s["ones_done"], 1)
            act.sem_inc(s["xcT_ready"], 1)
            act.sem_inc(s["h_done"], 2)
            act.sem_inc(s["res_ready"], 1)
            with act.Fori(0, PAIRS // CHUNK) as c:
                self_attention_act(act, c)
            act.wait_ge(s["ln_var"], 1)
            nc.scalar.activation(rstd[:, :], veps[:, :], ACT.Sqrt).then_inc(s["ln_std"], 1)
            for g in range(4):
                act.wait_ge(s["t_psum"], g + 1)
                nc.scalar.activation(xl2T[:, g * BANK:(g + 1) * BANK], bank(g % 2), ACT.Copy).then_inc(s["t_copied"], 1)
            for g in range(4):
                act.wait_ge(s["q2_psum"], g + 1)
                nc.scalar.activation(q2T[:, g * BANK:(g + 1) * BANK], bank(2 + g % 2), ACT.Copy).then_inc(s["q2_copied"], 1)

            def ctx_copies(p, par):
                for g in range(NG):
                    act.wait_ge(s["cT_psum1"], NG * p + (g + 1))
                    nc.scalar.activation(ctxT[par][:, 1, g, :], bank(4, 0, TG * ROWS), ACT.Copy).then_inc(s["cT_a"], 1)

            def prob_copies(p):
                for g in (0, 2):
                    act.wait_ge(s["p2T_psum"], NG * p + (g + 1))
                    nc.scalar.activation(prob2T[0:ROWS, g * TG:(g + 1) * TG, :],
                                         bank(5 + g % 2)[0:ROWS, :].rearrange("p (t n) -> p t n", t=TG),
                                         ACT.Copy).then_inc(s["p2T_a"], 1)

            def exps(p, par):
                act.wait_ge(s["m2_ready"], p + 1)
                nc.scalar.activation(prob2[par].rearrange("p (g m) -> p g m", g=NG), PS[:, 0:NG, 0:TG * ROWS], ACT.Exp,
                                     bias=nb2[:, 0:1], scale=0.25, accum_out=sum2[:, par:par + 1]).then_inc(s["p2_ready"], 1)

            def out_copy(p):
                act.wait_ge(s["o2_psum"], p + 1)
                nc.scalar.activation(oT, bank(7, 0, 128), ACT.Copy).then_inc(s["oT_ready"], 1)

            ctx_copies(0, 0)
            exps(0, 0)
            ctx_copies(1, 1)
            prob_copies(0)
            exps(1, 1)
            out_copy(0)
            def step(p, par):
                ctx_copies(p + 1, 1 - par)
                prob_copies(p)
                exps(p + 1, 1 - par)
                out_copy(p)
            with act.Fori(0, 3) as i:
                for j in range(4):
                    step(4 * i + (j + 1), (j + 1) % 2)
            step(13, 1)
            step(14, 0)
            prob_copies(15)
            out_copy(15)
            act.wait_ge(s["ln_var"], 2)
            nc.scalar.activation(rstd[:, :], veps[:, :], ACT.Sqrt).then_inc(s["ln_std"], 1)
            for g in range(4):
                act.wait_ge(s["t_psum"], 4 + 2 * g + 1)
                nc.scalar.activation(x2T[:, g * 448:(g + 1) * 448].rearrange("p (a t) -> p a t", t=T),
                                     bank(0).rearrange("p (a t) -> p a t", t=TP)[:, :, 0:T], ACT.Copy).then_inc(s["t_copied"], 1)
                act.wait_ge(s["t_psum"], 4 + 2 * g + 2)
                nc.scalar.activation(xlT[:, g * 448:(g + 1) * 448].rearrange("p (a t) -> p a t", t=T),
                                     bank(1).rearrange("p (a t) -> p a t", t=TP)[:, :, 0:T], ACT.Copy).then_inc(s["t_copied"], 1)
            act.wait_ge(s["bn_var"], 1)
            nc.scalar.activation(bsc[:, 1:2], bsc[:, 0:1], ACT.Sqrt).then_inc(s["bn_std"], 1)
            with act.Fori(0, 4) as i:
                for v in range(V):
                    act.wait_ge(s["h_psum"], V * i + (v + 1))
                    nc.scalar.activation(gelu[:, v, bass.ds(i * 448, 448)], bank(2 + v % 2, 0, 448), ACT.Gelu).then_inc(s["h_done"], 1)
            act.wait_ge(s["bn_ready"], 1)

            def normed(i, t):
                act.wait_ge(s["sim_psum"], 2 * i + (t + 1))
                nc.scalar.activation(xbn[:, t, :], xlT[:, bass.ds(i * 2 * TILE + t * TILE, TILE)], ACT.Identity,
                                     scale=bsc[:, 2:3], bias=bsc[:, 3:4]).then_inc(s["xbn_ready"], 1)

            def weights(i):
                for t in range(2):
                    act.wait_ge(s["best_ready"], 2 * i + (t + 1))
                    nc.scalar.activation(weight[:, t, :].rearrange("p (h k) -> p h k", h=NH), best[:, t], ACT.Sigmoid).then_inc(s["weight_ready"], 1)

            def rows(i):
                act.wait_ge(s["out_psum"], i + 1)
                act.wait_ge(s["out_done"], 16 * i + 16)
                nc.scalar.activation(res[:, :, :], bank(7, 0, 256).rearrange("p (t c) -> p t c", t=2), ACT.Copy).then_inc(s["res_ready"], 1)

            for t in range(2):
                normed(0, t)
            weights(0)
            for t in range(2):
                normed(1, t)
            with act.Fori(1, DUOS - 1) as i:
                weights(i)
                for t in range(2):
                    normed(i + 1, t)
                rows(i - 1)
            weights(DUOS - 1)
            rows(DUOS - 2)
            rows(DUOS - 1)

        @block.vector
        def _(dve):
            ch = Chain(dve, s["dve"])

            def layer_norm_stats(src):
                for p in range(PAIRS):
                    ch.did(nc.vector.bn_stats(stats[:, p, :], src[:, p, :]))
                ch.wait()
                for p in range(PAIRS):
                    ch.did(nc.vector.bn_aggr(mv[:, p, :], stats[:, p, :]))
                ch.wait()

            def layer_norm(src):
                ch.did(nc.vector.reciprocal(rstd[:, :], rstd[:, :]))
                ch.wait()
                for p in range(PAIRS):
                    last = ch.did(nc.vector.tensor_scalar(xn_[:, p, :], src[:, p, :], mv[:, p, 0:1], rstd[:, p:p + 1],
                                                          ALU.subtract, ALU.mult))
                ch.wait()

            dve.wait_ge(s["pads_zero"], 1)
            dve.wait_ge(s["x_in"], 32)
            layer_norm_stats(x0)
            nc.vector.tensor_scalar_add(veps[:, :], mv[:, :, 1], LN_EPS).then_inc(s["ln1_var"], 1)
            dve.wait_ge(s["ln1_std"], 1)
            layer_norm(x0)
            dve.sem_inc(s["ln1_done"], 1)
            dve.wait_ge(s["ka_in"], 16)
            ch.did(nc.vector.tensor_tensor(x0, x0, wa("bias1").rearrange("p (o c) -> p o c", o=1).to_broadcast([128, PAIRS, C]), ALU.add))
            ch.wait()
            dve.sem_inc(s["x1_done"], 1)

            def chunk(c):
                for n in range(2):
                    dve.wait_ge(s["qk_psum"], 2 * c + (n + 1))
                    for dst, b, k in ((rope_c, 0, "cos"), (rope_s, 1, "sin")):
                        ch.did(nc.vector.tensor_tensor(dst.rearrange("p (a n) -> p a n", a=CHUNK), bank(b).rearrange("p (a n) -> p a n", a=CHUNK),
                                                wa(k).rearrange("p (o n) -> p o n", o=1).to_broadcast([128, CHUNK, 128]), ALU.mult))
                    ch.wait()
                    dve.sem_inc(s["rope_read"], 1)
                    if n == 1:
                        dve.wait_ge(s["expanded"], 2 * c + 1)
                    nc.vector.tensor_tensor(rot, rope_c, rope_s, ALU.add).then_inc(s["rot_ready"], 1)
                    dve.wait_ge(s["rot_ready"], 2 * c + (n + 1))

                def softmax(j):
                    dve.wait_ge(s["s1_psum"], c * CHUNK + (j + 1))
                    S = PS[:, 2:4, :].rearrange("p b (h k) -> p (b h) k", k=TP)[:, :, 0:T]
                    ch.did(nc.vector.tensor_reduce(neg1[:, :], S, AX.X, ALU.max, negate=True))
                    ch.wait()
                    nc.vector.tensor_tensor(prob1[j % 2][:, :, 0:T], S, neg1[:, :].rearrange("p (h o) -> p h o", o=1).to_broadcast([128, HEADS, T]),
                                            ALU.add).then_inc(s["s1_read"], 1)

                def values(j):
                    dve.wait_ge(s["v_psum"], c * CHUNK + (j + 1))
                    nc.vector.tensor_tensor(vx.rearrange("p b h d -> p b (h d)"), bank(7, 0, 256).rearrange("p (b n) -> p b n", b=2),
                                            wa("vmask").rearrange("p (o n) -> p o n", o=1).to_broadcast([128, 2, C]),
                                            ALU.mult).then_inc(s["v_ready"], 1)

                def rest(j):
                    dve.wait_ge(s["p1_ready"], c * CHUNK + (j + 1))
                    ch.did(nc.vector.tensor_reduce(sum1[:, :], prob1[j % 2][:, :, 0:T], AX.X, ALU.add))
                    dve.wait_ge(s["p1T_psum"], 2 * (c * CHUNK) + 2 * j + 2)
                    nc.vector.tensor_copy(prob1T[:, 4:8, :], bank(5).rearrange("p (h n) -> p h n", h=4)).then_inc(s["p1T_b"], 1)
                    ch.wait()
                    ch.did(nc.vector.reciprocal(inv1[:, :], sum1[:, :]))
                    ch.wait()
                    dve.wait_ge(s["o1_psum"], c * CHUNK + (j + 1))
                    nc.vector.tensor_tensor(att.rearrange("p (h d) -> p h d", h=HEADS), bank(7, 256, 384).rearrange("p (h d) -> p h d", h=HEADS),
                                            inv1[:, :].rearrange("p (h o) -> p h o", o=1).to_broadcast([128, HEADS, HD]),
                                            ALU.mult).then_inc(s["att_ready"], 1)
                    dve.wait_ge(s["y1_psum"], c * CHUNK + (j + 1))
                    p = c * CHUNK + j
                    nc.vector.tensor_tensor(x1[:, bass.ds(p, 1), :], bank(6, 0, 128).rearrange("p (o n) -> p o n", o=1),
                                            x0[:, bass.ds(p, 1), :], ALU.add).then_inc(s["x1_done"], 1)

                for j in range(CHUNK):
                    softmax(j)
                    if j:
                        rest(j - 1)
                    values(j)
                rest(CHUNK - 1)

            PER = 4 + CHUNK * 3
            with dve.Fori(0, PAIRS // CHUNK) as c:
                ch.enter(c, PER)
                chunk(c)
            ch.leave(PAIRS // CHUNK)

            dve.wait_ge(s["x1_done"], PAIRS + 1)
            layer_norm_stats(x1)
            nc.vector.tensor_scalar_add(veps[:, :], mv[:, :, 1], LN_EPS).then_inc(s["ln_var"], 1)
            dve.wait_ge(s["ln_std"], 1)
            layer_norm(x1)
            dve.sem_inc(s["ln_done"], 1)
            ch.did(nc.vector.tensor_tensor(x1, x1, wa("bias2").rearrange("p (o c) -> p o c", o=1).to_broadcast([128, PAIRS, C]), ALU.add))
            ch.wait()
            dve.sem_inc(s["x2_done"], 1)

            def ctx_copies(p, par):
                for g in range(NG):
                    dve.wait_ge(s["cT_psum0"], NG * p + (g + 1))
                    nc.vector.tensor_copy(ctxT[par][:, 0, g, :], bank(3, 0, TG * ROWS)).then_inc(s["cT_d"], 1)

            def maximum(p):
                dve.wait_ge(s["s2_psum"], p + 1)
                ch.did(nc.vector.tensor_reduce(max2[:, :], PS[:, 0:NG, 0:TG * ROWS], AX.XY, ALU.max))
                ch.wait()
                nc.vector.tensor_scalar_mul(nb2[:, :], max2[:, :], -0.25).then_inc(s["m2_ready"], 1)

            def prob_copy(p, par):
                dve.wait_ge(s["p2_ready"], p + 1)
                nc.vector.reciprocal(inv2[:, par:par + 1], sum2[:, par:par + 1]).then_inc(s["dve"], 1)
                ch.n += 1
                dve.wait_ge(s["p2T_psum"], NG * p + 2)
                nc.vector.tensor_copy(prob2T[0:ROWS, TG:2 * TG, :],
                                      bank(6)[0:ROWS, :].rearrange("p (t n) -> p t n", t=TG)).then_inc(s["p2T_d"], 1)

            def residual(p, par):
                dve.wait_ge(s["y2_psum"], p + 1)
                ch.wait()
                nc.vector.scalar_tensor_tensor(x2[:, bass.ds(p, 1), :].rearrange("p o n -> p (o n)"), bank(7, 128, 256), inv2[:, par:par + 1],
                                               x1[:, bass.ds(p, 1), :].rearrange("p o n -> p (o n)"), ALU.mult, ALU.add).then_inc(s["x2_done"], 1)

            ctx_copies(0, 0)
            maximum(0)
            ctx_copies(1, 1)
            prob_copy(0, 0)
            maximum(1)

            def step(p, par):
                ctx_copies(p + 1, 1 - par)
                residual(p - 1, 1 - par)
                prob_copy(p, par)
                maximum(p + 1)
            with dve.Fori(0, 3) as i:
                ch.enter(i, 8)
                for j in range(4):
                    step(4 * i + (j + 1), (j + 1) % 2)
            ch.leave(3)
            step(13, 1)
            step(14, 0)
            residual(14, 0)
            prob_copy(15, 1)
            residual(15, 1)

            dve.wait_ge(s["x2_done"], PAIRS + 1)
            layer_norm_stats(x2)
            nc.vector.tensor_scalar_add(veps[:, :], mv[:, :, 1], LN_EPS).then_inc(s["ln_var"], 1)
            dve.wait_ge(s["ln_std"], 2)
            layer_norm(x2)
            dve.sem_inc(s["ln_done"], 1)
            for g in range(4):
                dve.wait_ge(s["t_copied"], 4 + 2 * g + 2)
                ch.did(nc.vector.bn_stats(bst[:, g, :], xlT[:, g * 448:(g + 1) * 448]))
            ch.wait()
            ch.did(nc.vector.bn_aggr(bmv[:, :], bst[:, :, :].rearrange("p a b -> p (a b)")))
            ch.wait()
            nc.vector.tensor_scalar_add(bsc[:, 0:1], bmv[:, 1:2], BN_EPS).then_inc(s["bn_var"], 1)
            dve.wait_ge(s["bn_std"], 1)
            ch.did(nc.vector.reciprocal(bsc[:, 0:1], bsc[:, 1:2]))
            ch.wait()
            ch.did(nc.vector.tensor_tensor(bsc[:, 2:3], bsc[:, 0:1], wa("gamma"), ALU.mult))
            ch.wait()
            ch.did(nc.vector.tensor_tensor(bsc[:, 0:1], bmv[:, 0:1], bsc[:, 2:3], ALU.mult))
            ch.wait()
            nc.vector.tensor_tensor(bsc[:, 3:4], wa("beta"), bsc[:, 0:1], ALU.subtract).then_inc(s["bn_ready"], 1)
            dve.sem_inc(s["sim_read"], 2)

            def best_keys(i, t):
                dve.wait_ge(s["sim_psum"], 2 * i + (2 + t + 1))
                dve.sem_inc(s["apart"], 1)
                v_t, i_t = val[:, t], idx[:, t]
                sim = bank(4 + t).rearrange("p (a h k) -> p a h k", a=2, h=NH)
                for a in range(2):
                    for h in range(NH):
                        ch.did(nc.vector.max(v_t[:, a, h, :], sim[:, a, h, :]))
                ch.wait_apart(s["apart"])
                for a in range(2):
                    for h in range(NH):
                        ch.did(nc.vector.max_index(i_t[:, a, h, :], v_t[:, a, h, :], sim[:, a, h, :]))
                at = 0
                spans = []
                for (a0, nb_), a1 in zip(PARTS, (1, 2, 4, 8)):
                    spans.append((a0, a1 - a0, nb_, at))
                    at += (a1 - a0) * nb_
                for a0, na_, nb_, at in spans:
                    ch.did(nc.vector.tensor_tensor(
                        cand[:, t, :, at:at + na_ * nb_].rearrange("p h (a b) -> p h a b", b=nb_),
                        v_t[:, 0, :, a0:a0 + na_].rearrange("p h (a o) -> p h a o", o=1).to_broadcast([128, NH, na_, nb_]),
                        v_t[:, 1, :, 0:nb_].rearrange("p h (o b) -> p h o b", o=1).to_broadcast([128, NH, na_, nb_]), ALU.add))
                ch.wait()
                dve.sem_inc(s["sim_read"], 1)
                ch.did(nc.vector.tensor_scalar_mul(idf[:, t, 0], i_t[:, 0], float(NK)))
                ch.did(nc.vector.tensor_copy(idf[:, t, 1], i_t[:, 1]))
                for h in range(NH):
                    ch.did(nc.vector.max(best[:, t, h, :], cand[:, t, h, :]))
                ch.wait()
                dve.sem_inc(s["best_ready"], 1)
                for a0, na_, nb_, at in spans:
                    ch.did(nc.vector.tensor_tensor(
                        cexp[:, t, :, at:at + na_ * nb_].rearrange("p h (a b) -> p h a b", b=nb_),
                        idf[:, t, 0, :, a0:a0 + na_].rearrange("p h (a o) -> p h a o", o=1).to_broadcast([128, NH, na_, nb_]),
                        idf[:, t, 1, :, 0:nb_].rearrange("p h (o b) -> p h o b", o=1).to_broadcast([128, NH, na_, nb_]), ALU.add))
                for h in range(NH):
                    ch.did(nc.vector.max_index(pos[:, t, h, :], best[:, t, h, :], cand[:, t, h, :]))
                ch.wait()
                ch.did(nc.vector.tensor_tensor(
                    hit[:, :, :, :], pos[:, t].rearrange("p h (o k) -> p h o k", o=1).to_broadcast([128, NH, NCAND, TOPK]),
                    iota_c[:, :, :].rearrange("p (o c) k -> p o c k", o=1).to_broadcast([128, NH, NCAND, TOPK]), ALU.is_equal))
                ch.wait()
                ch.did(nc.vector.tensor_tensor(
                    hite, hit[:, :, :, :],
                    cexp[:, t].rearrange("p h (c o) -> p h c o", o=1).to_broadcast([128, NH, NCAND, TOPK]), ALU.mult))
                ch.wait()
                ch.did(nc.vector.tensor_reduce(expert[:, t, :].rearrange("p (h k) -> p h k", h=NH),
                                               hite.rearrange("p h c k -> p h k c"), AX.X, ALU.add))

            def picks(i, first=False):
                dve.wait_ge(s["ew_psum"], i + 1)
                ch.did(nc.vector.tensor_copy(eT[:, :], bank(6, 0, 128)))
                ch.did(nc.vector.tensor_scalar_mul(w_hi[:, :], bank(6, 128, 256), W_UP))
                ch.wait()
                ch.did(nc.vector.scalar_tensor_tensor(w_lo[:, :], bank(6, 128, 256), W_UP, w_hi[:, :], ALU.mult, ALU.subtract))
                ch.did(nc.vector.tensor_single_scalar(eu[:, :], eT[:, :], EXPERTS - V, op=ALU.bitwise_and))
                ch.did(nc.vector.tensor_single_scalar(ev[:, :], eT[:, :], V - 1, op=ALU.bitwise_and))
                ch.wait()
                if not first:
                    dve.wait_ge(s["mix_psum"], i)
                ch.did(nc.vector.tensor_tensor(pick_v[:, :, :], ev[:, :].rearrange("p (o n) -> p o n", o=1).to_broadcast([128, V, TILE]),
                                               iota_v[:, :, :], ALU.is_equal))
                ch.did(nc.vector.tensor_tensor(pick_u, eu[:, :].rearrange("p (o n) -> p o n", o=1).to_broadcast([128, U, TILE]),
                                               iota_u, ALU.is_equal))
                ch.wait()
                for t in range(2):
                    for dst, w in ((b_hi, w_hi), (b_lo, w_lo)):
                        r = slice(t * HK, (t + 1) * HK)
                        ch.did(nc.vector.tensor_tensor(dst[r, t * V:(t + 1) * V, :], pick_v[r, :, :],
                                                       w[r, :].rearrange("p (o n) -> p o n", o=1).to_broadcast([HK, V, TILE]), ALU.mult))
                ch.wait()
                dve.sem_inc(s["picks"], 1)

            def mix(i):
                dve.wait_ge(s["mix_psum"], i + 1)
                for t in range(2):
                    for b in range(4):
                        src = bank(b).rearrange("p (n t v) -> p t v n", t=2, v=V)
                        ch.did(nc.vector.scalar_tensor_tensor(
                            act_w[:, t, :, b * 32:(b + 1) * 32], src[:, t], 1.0 / W_UP,
                            gelu[:, :, bass.ds(i * 2 * TILE + t * TILE + b * 32, 32)], ALU.mult, ALU.mult))
                ch.wait()
                dve.sem_inc(s["mixed"], 1)

            dve.wait_ge(s["iota_done"], 1)
            dve.wait_ge(s["h_done"], V * 4 + 2)

            def duo(i, first=False):
                for t in range(2):
                    best_keys(i, t)
                ch.wait()
                dve.sem_inc(s["expert_ready"], 1)
                picks(i, first)
            duo(0, True)
            with dve.Fori(0, DUOS - 1) as i:
                ch.enter(i, 2 * (16 + 16 + 4 + 2 + 8 + 4 + 8 + 3) + 5 + 2 + 4 + 8)
                duo(i + 1)
                mix(i)
            ch.leave(DUOS - 1)
            mix(DUOS - 1)

        @block.tensor
        def _(pe):
            mm = nc.tensor.matmul
            one = dict(start=True, stop=True)
            pe.wait_ge(s["ka_in"], 16)
            mm(bank(7, 0, 128), wa("xwq"), wa("xwk"), **one).then_inc(s["folded"], 1)
            mm(bank(6, 0, 128), wa("xwv"), wa("xproj"), **one).then_inc(s["folded"], 1)
            pe.wait_ge(s["kb_in"], 32)
            for n in range(2 * NH):
                last = mm(bank(5, n * NK, (n + 1) * NK), fwq[:, n * C:(n + 1) * C], wb("keys")[:, n * NK:(n + 1) * NK], **one)
            last.then_inc(s["folded"], 1)
            pe.wait_ge(s["fold_copied"], 3)

            def chunk(c):
                pe.wait_ge(s["xc_ready"], c + 1)
                pe.wait_ge(s["x1_done"], c * CHUNK + 1)
                for a in range(CHUNK):
                    last = nc.tensor.transpose(bank(6, a * 128, a * 128 + 128), xc[:, a, :], ident)
                last.then_inc(s["xcT_psum"], 1)
                pe.wait_ge(s["xcT_ready"], c + 2)
                for n, (w0, w1) in enumerate((("wq", "wqs"), ("wk", "wks"))):
                    if n:
                        pe.wait_ge(s["rope_read"], 2 * c + 1)
                    mm(bank(0), wa(w0), xcT, **one)
                    mm(bank(1), wa(w1), xcT, **one).then_inc(s["qk_psum"], 1)
                pe.wait_ge(s["expanded"], 2 * c + 2)

                def scores(j):
                    if j:
                        pe.wait_ge(s["s1_read"], c * CHUNK + j)
                    for g in range(4):
                        for b in range(2):
                            at = j * 128 + b * TP
                            o = PS[b * TP:(b + 1) * TP, 2 + g // 2, (g % 2) * 256:(g % 2) * 256 + 256].rearrange("p (h k) -> p h k", k=TP)[:, :, 0:T]
                            last = mm(o, qx[:, g, at:at + TP], kx[:, :, at:at + T], **one)
                    last.then_inc(s["s1_psum"], 1)
                    if j:
                        pe.wait_ge(s["v_ready"], c * CHUNK + j)
                    else:
                        pe.wait_ge(s["xcT2_ready"], c + 1)
                    for b in range(2):
                        last = mm(bank(7, b * 128, b * 128 + 128), xcT2[:, 2 * j + b].rearrange("p r n -> p (r n)"), wa("wv"), **one)
                    last.then_inc(s["v_psum"], 1)

                def rest(j):
                    P = c * CHUNK + j
                    pe.wait_ge(s["p1_ready"], c * CHUNK + (j + 1))
                    for h in range(HEADS // 2):
                        last = nc.tensor.transpose(bank(4 + h // 4, (h % 4) * 128, (h % 4) * 128 + 128),
                                                   prob1[j % 2][:, 2 * h:2 * h + 2, :].rearrange("p h k -> p (h k)"), ident)
                        if h % 4 == 3:
                            last.then_inc(s["p1T_psum"], 1)
                    pe.wait_ge(s["p1T_a"], c * CHUNK + (j + 1))
                    pe.wait_ge(s["p1T_b"], c * CHUNK + (j + 1))
                    pe.wait_ge(s["v_ready"], c * CHUNK + (j + 1))
                    for h in range(HEADS // 2):
                        for b in range(2):
                            last = mm(bank(7, 256 + h * 16, 256 + h * 16 + 16)[b * TP:(b + 1) * TP, :],
                                      prob1T[:, h, b * TP:(b + 1) * TP], vx[:, b, h, :], **one)
                    last.then_inc(s["o1_psum"], 1)
                    pe.wait_ge(s["att_ready"], c * CHUNK + (j + 1))
                    nc.tensor.transpose(bank(7, 384, 512), att, ident).then_inc(s["attT_psum"], 1)
                    pe.wait_ge(s["attT_ready"], c * CHUNK + (j + 1))
                    pe.wait_ge(s["x1_done"], c * CHUNK + (j + 1))
                    mm(bank(6, 0, 128), attT, wa("wproj"), **one).then_inc(s["y1_psum"], 1)

                for j in range(CHUNK):
                    scores(j)
                    if j:
                        rest(j - 1)
                rest(CHUNK - 1)

            with pe.Fori(0, PAIRS // CHUNK) as c:
                chunk(c)

            pe.wait_ge(s["ln_done"], 1)
            for g in range(4):
                if g >= 2:
                    pe.wait_ge(s["t_copied"], g - 1)
                for a in range(4):
                    last = nc.tensor.transpose(bank(g % 2, a * 128, a * 128 + 128), xn_[:, 4 * g + a, :], ident)
                last.then_inc(s["t_psum"], 1)
            for g in range(4):
                pe.wait_ge(s["t_copied"], g + 1)
                if g >= 2:
                    pe.wait_ge(s["q2_copied"], g - 1)
                mm(bank(2 + g % 2), A2[:, :], xl2T[:, g * BANK:(g + 1) * BANK], **one).then_inc(s["q2_psum"], 1)
            pe.wait_ge(s["q2_copied"], 4)

            def ctx_transposes(p, slot):
                slot_use = p // RING + 1 if isinstance(p, int) else None
                for g in range(NG):
                    for b in range(2):
                        if g:
                            pe.wait_ge(s["cT_d" if b == 0 else "cT_a"], NG * p + g)
                        for k in range(TG):
                            last = nc.tensor.transpose(bank(3 + b, k * ROWS, (k + 1) * ROWS), ring[slot][0:ROWS, b, g * TG + k, :],
                                                       ident[0:ROWS, 0:ROWS])
                        last.then_inc(s[f"cT_psum{b}"], 1)

            def scores(p, par):
                pe.wait_ge(s["q2_ready"], p + 1)
                for g in range(NG):
                    pe.wait_ge(s["cT_d"], NG * p + (g + 1))
                    pe.wait_ge(s["cT_a"], NG * p + (g + 1))
                    for b in range(2):
                        last = mm(PS[b * TP:(b + 1) * TP, g, 0:TG * ROWS], q2[par][:, b * TP:(b + 1) * TP], ctxT[par][:, b, g, :], **one)
                last.then_inc(s["s2_psum"], 1)

            def products(p, par, slot):
                pe.wait_ge(s["p2_ready"], p + 1)
                for g in range(NG):
                    if g == 2:
                        pe.wait_ge(s["p2T_a"], 2 * p + 1)
                    for k in range(TG):
                        t = g * TG + k
                        last = nc.tensor.transpose(bank(5 + g % 2, k * 128, k * 128 + 128)[0:ROWS, :],
                                                   prob2[par][:, t * ROWS:(t + 1) * ROWS], ident)
                    last.then_inc(s["p2T_psum"], 1)
                pe.wait_ge(s["p2T_a"], 2 * p + 2)
                pe.wait_ge(s["p2T_d"], p + 1)
                for b in range(2):
                    for t in range(NT):
                        last = mm(bank(7, b * TP, (b + 1) * TP), ring[slot][0:ROWS, b, t, :], prob2T[0:ROWS, t, b * TP:(b + 1) * TP],
                                  start=t == 0, stop=t == NT - 1)
                last.then_inc(s["o2_psum"], 1)

            def project(p):
                pe.wait_ge(s["oT_ready"], p + 1)
                pe.wait_ge(s["x2_done"], p + 1)
                mm(bank(7, 128, 256), oT, Wvp[:, :], **one).then_inc(s["y2_psum"], 1)

            def arrived(slot, use):
                pe.wait_ge(s[f"ctx{slot}"], 32 * use)

            arrived(0, 1)
            ctx_transposes(0, 0)
            scores(0, 0)
            arrived(1, 1)
            ctx_transposes(1, 1)
            scores(1, 1)
            products(0, 0, 0)

            def step(p, par, slot, use):
                arrived((slot + 1) % RING, use)
                ctx_transposes(p + 1, (slot + 1) % RING)
                project(p - 1)
                scores(p + 1, 1 - par)
                products(p, par, slot)
            with pe.Fori(0, 3) as i:
                for j in range(4):
                    step(4 * i + (j + 1), (j + 1) % 2, (j + 1) % RING, i + (1 + (j + 2) // RING))
            step(13, 1, 1, 4)
            step(14, 0, 2, 4)
            project(14)
            products(15, 1, 3)
            project(15)

            pe.wait_ge(s["ln_done"], 2)
            for g in range(4):
                for n, src in enumerate((x2, xn_)):
                    if g:
                        pe.wait_ge(s["t_copied"], 4 + 2 * (g - 1) + n + 1)
                    for a in range(4):
                        last = nc.tensor.transpose(bank(n, a * 128, a * 128 + 128), src[:, 4 * g + a, :], ident)
                    last.then_inc(s["t_psum"], 1)
            pe.wait_ge(s["t_copied"], 12)
            with pe.Fori(0, 4) as i:
                for v in range(V):
                    pe.wait_ge(s["h_done"], V * i + (v + 1))
                    mm(bank(2 + v % 2, 0, 448), wb("down")[:, v * U:(v + 1) * U], xlT[:, bass.ds(i * 448, 448)], **one).then_inc(s["h_psum"], 1)
            pe.wait_ge(s["h_done"], V * 4 + 2)
            pe.sem_inc(s["sim_psum"], 2)

            def key_scores(i):
                for t in range(2):
                    pe.wait_ge(s["xbn_ready"], 2 * i + (t + 1))
                    pe.wait_ge(s["sim_read"], 2 * i + (t + 1))
                    mm(bank(4 + t), xbn[:, t, :], Wsim[:, :], **one).then_inc(s["sim_psum"], 1)

            def expert_transposes(i):
                pe.wait_ge(s["expert_ready"], i + 1)
                nc.tensor.transpose(bank(6, 0, 128), expert[:, :, :].rearrange("p t k -> p (t k)"), ident)
                pe.wait_ge(s["weight_ready"], 2 * i + 2)
                nc.tensor.transpose(bank(6, 128, 256), weight[:, :, :].rearrange("p t k -> p (t k)"), ident).then_inc(s["ew_psum"], 1)

            def spread(i):
                pe.wait_ge(s["picks"], i + 1)
                for n in range(TILE):
                    o = bank(n // 32, (n % 32) * 16, (n % 32) * 16 + 16)
                    mm(o, pick_u[:, :, n], b_hi[:, :, n], start=True, stop=False)
                    last = mm(o, pick_u[:, :, n], b_lo[:, :, n], start=False, stop=True)
                last.then_inc(s["mix_psum"], 1)

            def gather(i):
                pe.wait_ge(s["mixed"], i + 1)
                pe.wait_ge(s["x2s_ready"], i + 1)
                pe.wait_ge(s["res_ready"], i + 1)
                for t in range(2):
                    o = bank(7, t * 128, t * 128 + 128)
                    mm(o, x2s[:, t, :], ident, start=True, stop=False)
                    for v in range(V):
                        last = mm(o, act_w[:, t, v, :], wb("up")[:, v * C:(v + 1) * C], start=False, stop=v == V - 1)
                last.then_inc(s["out_psum"], 1)

            key_scores(0)
            expert_transposes(0)
            key_scores(1)
            spread(0)
            with pe.Fori(1, DUOS - 1) as i:
                expert_transposes(i)
                gather(i - 1)
                key_scores(i + 1)
                spread(i)
            expert_transposes(DUOS - 1)
            gather(DUOS - 2)
            spread(DUOS - 1)
            gather(DUOS - 1)


def constants():
    import numpy as np
    p = np.arange(128)
    inv = (1.0 / 10000.0 ** (np.arange(0, HD, 2, dtype=np.float32) / np.float32(HD))).astype(np.float32)
    ang = np.arange(T, dtype=np.float32)[None, :] * inv[(p % HD) // 2][:, None]
    cos = np.zeros((128, 2, TP), np.float32)
    sin = np.zeros((128, 2, TP), np.float32)
    cos[:, :, :T] = np.cos(ang)[:, None, :]
    sin[:, :, :T] = np.where(p % 2 == 0, -1.0, 1.0)[:, None, None] * np.sin(ang)[:, None, :]
    four = np.arange(4)
    col = np.arange(C)
    return {
        "ident": np.eye(128, dtype=np.float32),
        "cos": cos.reshape(128, 2 * TP).astype(np.float32), "sin": sin.reshape(128, 2 * TP).astype(np.float32),
        "slot": ((p // HD % 4)[:, None] == four).astype(np.float32),
        "group": ((p // 32)[:, None] == four).astype(np.float32),
        "vmask": ((p // TP)[:, None] == (col // HD % 2)[None, :]).astype(np.float32),
    }


def kernel(**inputs):
    import numpy as np
    import concourse.bacc as bacc
    from concourse.bass_utils import run_bass_kernel_spmd

    a = {k: np.asarray(v) for k, v in inputs.items()}
    qkv = a["L0_attn_w_qkv"]
    swapped = qkv.reshape(3 * C // 2, 2, C)[:, ::-1].reshape(3 * C, C)
    row = lambda b: np.broadcast_to(b[None, :], (128, C))
    cols = {
        "wq": qkv[:C].T, "wqs": swapped[:C].T, "wk": qkv[C:2 * C].T, "wks": swapped[C:2 * C].T, "wv": qkv[2 * C:].T,
        "wproj": a["L0_attn_w_proj"].T,
        "xwq": a["L0_xattn_wq"].T, "xwk": a["L0_xattn_wk"].T, "xwv": a["L0_xattn_wv"].T, "xproj": a["L0_xattn_w_proj"],
        "bias1": row(a["L0_attn_b_proj"]), "bias2": row(a["L0_xattn_b_proj"]),
        "gamma": a["L0_ffn_bn_gamma"][:, None], "beta": a["L0_ffn_bn_beta"][:, None],
        "keys": a["L0_ffn_keys_p"].transpose(3, 2, 0, 1).reshape(C, -1),
        "down": a["L0_ffn_down"][:EXPERTS].reshape(U, V, C).transpose(2, 1, 0).reshape(C, -1),
        "up": a["L0_ffn_up"][:EXPERTS].reshape(U, V * C),
        **constants(),
    }
    arrays = {
        "x": np.ascontiguousarray(a["x"]), "ctx": np.ascontiguousarray(a["ctx_1024"]),
        "pack_a": np.ascontiguousarray(np.concatenate([cols[n] for n, _ in PACK_A], axis=1)),
        "pack_b": np.ascontiguousarray(np.concatenate([cols[n] for n, _ in PACK_B], axis=1)),
        "pack_q": np.ascontiguousarray(a["L0_ffn_w_q"].reshape(2 * NH, C, C).transpose(1, 0, 2).reshape(C, -1)),
    }
    nc = bacc.Bacc("TRN2", target_bir_lowering=False, num_devices=1)
    args = [nc.dram_tensor(n, v.shape, mybir.dt.from_np(v.dtype), kind="ExternalInput").ap() for n, v in arrays.items()]
    out = nc.dram_tensor("out", (B, T, C), F32, kind="ExternalOutput").ap()
    decoder_block(nc, *args, out)
    r = run_bass_kernel_spmd(nc, [arrays], core_ids=[0])
    return r.results[0]["out"]
```

```python
import concourse.bass as bass
from concourse import mybir
from contextlib import ExitStack

F32 = mybir.dt.float32
F16 = mybir.dt.float16
U16 = mybir.dt.uint16
ALU = mybir.AluOpType
ACT = mybir.ActivationFunctionType
AX = mybir.AxisListType

B, T, C = 32, 56, 128
CTX = 1500
HEADS, HD = 16, 8
NH, NK, TOPK = 8, 32, 8
TP = 64
PAIRS = B // 2
AHEAD = 3
LOOPED = PAIRS - 2 * AHEAD
TOK = B * T
VW = 2 * HD + 2
ROWS = 125
NT = CTX // ROWS
BANK = 512
TG = 4
NG = NT // TG
SPREAD = 112
RING = 4
TILE = 128
DUOS = TOK // (2 * TILE)
EXPERTS = NK * NK
U, V = 128, 8
HK = NH * TOPK
NCAND = 20
SPANS = ((0, 1, 8, 0), (1, 1, 4, 8), (2, 2, 2, 12), (4, 4, 1, 16))
LN_EPS = 1e-5
BN_EPS = 1e-5
W_UP = 16384.0

PACK_A = [("wq", C), ("wqs", C), ("wk", C), ("wks", C), ("wv", C), ("wproj", C),
          ("xwq", C), ("xwk", C), ("xwv", C), ("xproj", C), ("ident", C), ("cos", 2 * TP), ("sin", 2 * TP),
          ("slot", 4), ("group", 4), ("bias1", C), ("bias2", C), ("gamma", 1), ("beta", 1)]
PACK_B = [("keys", 2 * NH * NK), ("down", EXPERTS), ("up", EXPERTS)]


def columns(pack):
    at, out = 0, {}
    for name, n in pack:
        out[name] = (at, at + n)
        at += n
    return out, at


class Chain:

    def __init__(self, eng, sem):
        self.eng, self.sem, self.base, self.n = eng, sem, 0, 0

    def did(self, ins):
        ins.then_inc(self.sem, 1)
        self.n += 1
        return ins

    def wait(self):
        self.eng.wait_ge(self.sem, self.base + self.n)

    def wait_apart(self, stand):
        self.wait()
        self.eng.sem_inc(stand, 1)

    def enter(self, i, per_pass):
        self.start, self.per_pass = self.n, per_pass
        self.base = i * per_pass

    def leave(self, passes):
        assert self.n - self.start == self.per_pass, (self.n - self.start, self.per_pass)
        self.n, self.base = self.start + self.per_pass * passes, 0


def decoder_block(nc, x, ctx, pack_a, pack_b, pack_q, out):
    ca, na = columns(PACK_A)
    cb, nb = columns(PACK_B)
    with ExitStack() as stack:
        def sb(name, shape, dt=F32):
            return stack.enter_context(nc.sbuf_tensor(name, shape, dt))

        def sem(name):
            return stack.enter_context(nc.semaphore(name))

        KA = sb("KA", [128, na])
        KB = sb("KB", [128, nb])
        def wa(name):
            return KA[:, ca[name][0]:ca[name][1]]
        def wb(name):
            return KB[:, cb[name][0]:cb[name][1]]
        ident = wa("ident")

        XA = sb("XA", [128, 4 * PAIRS * C])
        def xpart(n):
            return XA[:, n * PAIRS * C:(n + 1) * PAIRS * C].rearrange("p (a c) -> p a c", c=C)
        x0 = xpart(0)
        xl2T = XA[:, PAIRS * C:2 * PAIRS * C]
        x1 = xpart(2)
        q2T = XA[:, 3 * PAIRS * C:4 * PAIRS * C]
        iota_u = XA[:, 0:U // 2 * TILE // 2].bitcast(U16).rearrange("p (u n) -> p u n", n=TILE)
        xn_ = sb("xn", [128, PAIRS, C])
        x2 = sb("x2", [128, PAIRS, C])
        x2T = sb("x2T", [128, TOK])
        xlT = sb("xlT", [128, TOK])
        stats = sb("stats", [128, PAIRS, 6])
        mv = sb("mv", [128, PAIRS, 2])
        rstd = sb("rstd", [128, PAIRS])
        veps = sb("veps", [128, PAIRS])
        A2 = sb("A2", [128, C])
        Wvp = sb("Wvp", [128, C])
        Wsim = sb("Wsim", [128, 2 * NH * NK])

        CTXF = 2 * NT * C
        ARENA = RING * CTXF + 2 * CTXF + 2 * CTX + NT * 128 + 1536
        AR = sb("AR", [128, ARENA])
        used = [0]
        def take(n):
            at = used[0]
            used[0] += n
            assert used[0] <= ARENA, (used[0], ARENA)
            return AR[:, at:at + n]
        ring = [take(CTXF).rearrange("p (b t c) -> p b t c", b=2, t=NT) for _ in range(RING)]
        after_ring = used[0]
        ctxT = [take(2 * CTX).rearrange("p (b g m) -> p b g m", b=2, g=NG) for _ in range(2)]
        prob2 = [take(CTX) for _ in range(2)]
        prob2T = take(NT * 128).rearrange("p (t n) -> p t n", t=NT)
        q2 = [take(128) for _ in range(2)]
        o2 = take(128)
        oT = take(128)
        used[0] = after_ring
        xc = [take(C) for _ in range(2)]
        xcT = [take(128) for _ in range(2)]
        rope = take(4 * 128)
        rot_q = take(128)
        rot_k = take(128)
        qx = [take(4 * 128).rearrange("p (g n) -> p g n", g=4) for _ in range(2)]
        kx = [take(4 * 128).rearrange("p (g n) -> p g n", g=4) for _ in range(2)]
        prob1 = [take(HEADS * TP).rearrange("p (h k) -> p h k", h=HEADS) for _ in range(2)]
        prob1T = take(HEADS // 2 * 128).rearrange("p (h n) -> p h n", n=128)
        vx = [take(2 * HEADS // 2 * VW).rearrange("p (b h d) -> p b h d", b=2, d=VW) for _ in range(2)]
        att = take(C)
        attT = take(C)
        fwq = take(2 * NH * C)
        used[0] = 0
        gelu = take(V * TOK).rearrange("p (v n) -> p v n", v=V)
        pick_u = take(U * TILE // 2).bitcast(F16).rearrange("p (u n) -> p u n", u=U)
        neg1 = sb("neg1", [128, HEADS])
        inv1 = sb("inv1", [128, HEADS])
        max2 = sb("max2", [128, 1])
        nb2 = sb("nb2", [128, 1])
        sum2 = sb("sum2", [128, 2])
        inv2 = sb("inv2", [128, 2])
        bst = sb("bst", [128, 4, 6])
        bmv = sb("bmv", [128, 2])
        bsc = sb("bsc", [128, 4])
        spare = sb("spare", [128, 2])
        xbn = sb("xbn", [128, 2, TILE])
        x2s = sb("x2s", [128, 2, TILE])
        val = sb("val", [128, 2, 2, NH, TOPK])
        idx = sb("idx", [128, 2, 2, NH, TOPK], U16)
        idf = sb("idf", [128, 2, 2, NH, TOPK])
        cand = sb("cand", [128, 2, NH, NCAND])
        cexp = sb("cexp", [128, NCAND, 2, NH])
        best = sb("best", [128, 2, NH, TOPK])
        pos = sb("pos", [128, 2, NH, TOPK], U16)
        hit = xn_[:, :, :].rearrange("p a c -> p (a c)")[:, 0:NCAND * HK].bitcast(F16).rearrange("p (c t k) -> p c t k", c=NCAND, t=2)
        ident16 = sb("ident16", [128, 128], F16)
        weight = sb("weight", [128, 2, HK])
        eT = sb("eT", [128, TILE], U16)
        eu = sb("eu", [128, 2, TILE], U16)
        ev = sb("ev", [128, TILE], U16)
        w_hi = sb("w_hi", [128, TILE], F16)
        w_lo = sb("w_lo", [128, TILE], F16)
        pick_v = sb("pick_v", [128, V, TILE], F16)
        b_hi = sb("b_hi", [128, 2 * V, TILE], F16)
        b_lo = sb("b_lo", [128, 2 * V, TILE], F16)
        act_w = x2[:, :, :].rearrange("p a c -> p (a c)").rearrange("p (t v n) -> p t v n", t=2, v=V)
        iota_v = sb("iota_v", [128, V, TILE], U16)
        iota_c = sb("iota_c", [128, NCAND, HK], U16)
        res = sb("res", [128, 2, C])

        PS = stack.enter_context(nc.psum_tensor("PS", [128, 8, BANK], F32))
        Q_BANKS = (2, 7)
        T_BANKS = ((3, 4), (5, 6), (3, 4))
        P_BANKS = (5, 6, 3)

        def bank(n, a=0, b=BANK):
            return PS[:, n, a:b]

        s = {n: sem(n) for n in (
            "x_in ka_in kb_in out_done ctx0 ctx1 ctx2 ctx3 "
            "dve pool apart apart_pool pads_zero zeros_done folded fold_copied "
            "ln1_var ln1_std xc_ready xcT_psum xcT_ready qk_psum rope_ready rot_q_ready kx_ready qx_ready bias_added "
            "s1_psum s1_read v_psum vx_ready p1_ready p1T_psum p1T_ready o1_psum att_ready attT_psum attT_ready "
            "y1_psum x1_done "
            "ln_var ln_std ln_done t_psum t_copied q2_psum q2_copied q2_ready "
            "cT_psum0 cT_psum1 cT_a cT_d s2_psum m2_ready p2_ready p2T_psum p2T_a p2T_d o2_psum o2_ready o2T_psum oT_ready y2_psum x2_done "
            "bn_var bn_std bn_ready h_psum h_done iota_done "
            "xbn_ready sim_psum sim_read best_ready weight_ready index_ready hit_ready expert_ready "
            "x2s_ready ew_psum ew_read picks mix_psum mixed out_psum res_ready").split()}
        block = stack.enter_context(nc.Block())

        @block.sync
        def _(sp):
            sp.sem_inc(s["out_done"], 16)
            rows_out = out.rearrange("b t c -> (b t) c")
            sp.dma_start(KA[:, :], pack_a).then_inc(s["ka_in"], 16)
            for b in range(2):
                sp.wait_ge(s["pads_zero"], 2)
                sp.dma_start(x0[b * TP:b * TP + T, :, :],
                             x.rearrange("(a b) t c -> b t a c", b=2)[b]).then_inc(s["x_in"], 16)
            sp.dma_start(KB[:, :], pack_b).then_inc(s["kb_in"], 16)
            sp.dma_start(fwq, pack_q).then_inc(s["kb_in"], 16)

            def load(p, slot):
                src = ctx[bass.ds(2 * p, 2), :, :].rearrange("b (p t) c -> p b t c", t=NT)
                for a, z in ((0, SPREAD), (SPREAD, ROWS)):
                    sp.dma_start(ring[slot][a:z], src[a:z]).then_inc(s[f"ctx{slot}"], 16)

            for p in range(RING):
                load(p, p)
            with sp.Fori(0, PAIRS // RING - 1) as i:
                for j in range(RING):
                    sp.wait_ge(s["o2_psum"], i * RING + (j + 1))
                    load((i + 1) * RING + j, j)
            with sp.Fori(0, DUOS) as i:
                sp.wait_ge(s["res_ready"], i + 2)
                sp.dma_start(rows_out[bass.ds(i * 2 * TILE, 2 * TILE), :].rearrange("(t p) c -> p t c", p=TILE),
                             res[:, :, :]).then_inc(s["out_done"], 16)
            sp.wait_ge(s["out_done"], 16 * DUOS + 16)

        @block.gpsimd
        def _(pool):
            ch = Chain(pool, s["pool"])
            ch.did(nc.gpsimd.memset(x0[32:64, :, :], 0.0))
            ch.wait()
            pool.sem_inc(s["pads_zero"], 1)
            for n in range(2):
                ch.did(nc.gpsimd.memset(prob1[n][:, :, T:TP], 0.0))
                ch.did(nc.gpsimd.memset(vx[n], 0.0))
            ch.wait()
            for n in range(2):
                ch.did(nc.gpsimd.memset(vx[n][0:TP, :, :, 2 * HD:2 * HD + 1], 1.0))
            ch.wait()
            for n in range(2):
                ch.did(nc.gpsimd.memset(vx[n][TP:128, :, :, 2 * HD + 1:VW], 1.0))
            ch.wait()
            pool.sem_inc(s["zeros_done"], 1)
            pool.wait_ge(s["ka_in"], 16)
            pool.wait_ge(s["x_in"], 32)

            def rotate(p, par):
                pool.wait_ge(s["rope_ready"], p + 1)
                pool.sem_inc(s["apart_pool"], 1)
                nc.gpsimd.tensor_tensor(rot_q, rope[:, 0:128], rope[:, 256:384], ALU.add).then_inc(s["rot_q_ready"], 1)
                pool.wait_ge(s["rot_q_ready"], p + 1)
                pool.sem_inc(s["apart_pool"], 1)
                nc.gpsimd.tensor_tensor(qx[par], rot_q.rearrange("p (o n) -> p o n", o=1).to_broadcast([128, 4, 128]),
                                        wa("group").rearrange("p (g o) -> p g o", o=1).to_broadcast([128, 4, 128]), ALU.mult).then_inc(s["qx_ready"], 1)
                nc.gpsimd.tensor_tensor(x1[:, bass.ds(p, 1), :], x0[:, bass.ds(p, 1), :],
                                        wa("bias1").rearrange("p (o c) -> p o c", o=1), ALU.add).then_inc(s["bias_added"], 1)
                pool.wait_ge(s["qx_ready"], p + 1)
                pool.sem_inc(s["apart_pool"], 1)
            rotate(0, 0)
            rotate(1, 1)
            with pool.Fori(1, PAIRS // 2) as i:
                for j in range(2):
                    rotate(2 * i + j, j)
            ch.did(nc.gpsimd.memset(b_hi[:, :, :], 0.0))
            ch.did(nc.gpsimd.memset(b_lo[:, :, :], 0.0))
            ch.did(nc.gpsimd.iota(iota_v[:, :, :], pattern=[[1, V], [0, TILE]], base=0, channel_multiplier=0))
            ch.did(nc.gpsimd.iota(iota_c[:, :, :], pattern=[[1, NCAND], [0, HK]], base=0, channel_multiplier=0))
            ch.did(nc.gpsimd.tensor_copy(ident16[:, :], ident))
            ch.wait()
            pool.wait_ge(s["q2_copied"], 1)
            for p in range(2):
                nc.gpsimd.tensor_copy(q2[p], q2T[:, p * 128:(p + 1) * 128]).then_inc(s["q2_ready"], 1)
            pool.wait_ge(s["q2_copied"], 4)
            nc.gpsimd.iota(iota_u, pattern=[[V, U // 2], [0, TILE]], base=0, channel_multiplier=0).then_inc(s["iota_done"], 1)
            with pool.Fori(0, PAIRS // 2 - 1) as i:
                for j in range(2):
                    pool.wait_ge(s["s2_psum"], 2 * i + (j + 1))
                    pool.sem_inc(s["apart_pool"], 1)
                    nc.gpsimd.tensor_copy(q2[j], q2T[:, bass.ds((2 * i + 2 + j) * 128, 128)]).then_inc(s["q2_ready"], 1)
            def experts(i, t):
                pool.wait_ge(s["index_ready"], 2 * i + (t + 1))
                pool.sem_inc(s["apart_pool"], 1)
                ch.did(nc.gpsimd.tensor_scalar(idf[:, t, 0], idx[:, t, 0], float(NK), 0.0, ALU.mult, ALU.add))
                ch.did(nc.gpsimd.tensor_copy(idf[:, t, 1], idx[:, t, 1]))
                ch.wait()
                for a0, na_, nb_, at in SPANS:
                    ch.did(nc.gpsimd.tensor_tensor(
                        cexp[:, at:at + na_ * nb_, t, :].rearrange("p (a b) h -> p a b h", b=nb_),
                        idf[:, t, 0, :, a0:a0 + na_].rearrange("p h (a o) -> p a o h", o=1).to_broadcast([128, na_, nb_, NH]),
                        idf[:, t, 1, :, 0:nb_].rearrange("p h (o b) -> p o b h", o=1).to_broadcast([128, na_, nb_, NH]), ALU.add))
                ch.wait()
                pool.wait_ge(s["hit_ready"], 2 * i + (t + 1))
                h4 = hit[:, :, t, :].rearrange("p c (h k) -> p c h k", h=NH)
                nc.gpsimd.tensor_tensor(h4, h4, cexp[:, :, t, :].rearrange("p c (h o) -> p c h o", o=1).to_broadcast([128, NCAND, NH, TOPK]),
                                        ALU.mult).then_inc(s["expert_ready"], 1)

            def residual(i):
                for t in range(2):
                    last = nc.gpsimd.tensor_copy(x2s[:, t, :], x2T[:, bass.ds(i * 2 * TILE + t * TILE, TILE)])
                last.then_inc(s["x2s_ready"], 1)
            pool.wait_ge(s["t_copied"], 8)
            residual(0)
            experts(0, 0)
            experts(0, 1)
            with pool.Fori(0, DUOS - 1) as i:
                ch.enter(i, 12)
                experts(i + 1, 0)
                experts(i + 1, 1)
                pool.wait_ge(s["out_psum"], i + 1)
                pool.sem_inc(s["apart_pool"], 1)
                residual(i + 1)
            ch.leave(DUOS - 1)

        def within(p):
            return not isinstance(p, int) or 0 <= p < PAIRS

        def after(p, n):
            return not isinstance(p, int) or p >= n

        def self_attention(eng, step, chain=None, per_pass=0):
            for p in range(-AHEAD, AHEAD):
                step(p, p % 2)
            with eng.Fori(0, LOOPED // 2) as i:
                if chain:
                    chain.enter(i, per_pass)
                for j in range(2):
                    step(2 * i + (AHEAD + j), (AHEAD + j) % 2)
            if chain:
                chain.leave(LOOPED // 2)
            for p in range(AHEAD + LOOPED, PAIRS + 2):
                step(p, p % 2)

        @block.scalar
        def _(act):
            def table_ahead(n):
                nc.scalar.activation(spare[:, n:n + 1], ident[:, 0:1], ACT.Sqrt)

            act.wait_ge(s["ln1_var"], 1)
            nc.scalar.activation(rstd[:, :], veps[:, :], ACT.Sqrt).then_inc(s["ln1_std"], 1)
            act.sem_inc(s["res_ready"], 1)
            act.wait_ge(s["zeros_done"], 1)

            def softmax(p, par):
                act.wait_ge(s["s1_read"], p + 1)
                nc.scalar.activation(prob1[par][:, :, 0:T], prob1[par][:, :, 0:T], ACT.Exp, scale=HD ** -0.5).then_inc(s["p1_ready"], 1)

            def att_copy(p):
                act.wait_ge(s["attT_psum"], p + 1)
                nc.scalar.activation(attT, bank(7, 0, 128), ACT.Copy).then_inc(s["attT_ready"], 1)

            def values(p, par):
                act.wait_ge(s["v_psum"], p + 1)
                for a in range(2):
                    r = slice(a * TP, (a + 1) * TP)
                    nc.scalar.activation(vx[par][r, :, :, a * HD:(a + 1) * HD], bank(5, 0, 128)[r].rearrange("p (b h d) -> p b h d", b=2, d=HD),
                                         ACT.Copy).then_inc(s["vx_ready"], 1)

            def row_copy(p, par):
                act.wait_ge(s["xcT_psum"], p + 1)
                nc.scalar.activation(xcT[par], bank(6, 256, 384), ACT.Copy).then_inc(s["xcT_ready"], 1)

            def prob_copy(p):
                for g in range(2):
                    act.wait_ge(s["p1T_psum"], 2 * p + (g + 1))
                    nc.scalar.activation(prob1T[:, 4 * g:4 * g + 4, :], bank(3 + g).rearrange("p (h n) -> p h n", h=4), ACT.Copy).then_inc(s["p1T_ready"], 1)

            def step(p, par):
                if within(p - 1):
                    softmax(p - 1, 1 - par)
                if within(p - 2):
                    att_copy(p - 2)
                if within(p):
                    values(p, par)
                if within(p + 2):
                    row_copy(p + 2, par)
                if within(p - 1):
                    prob_copy(p - 1)
                if isinstance(p, int) and p == PAIRS:
                    for n, (dst, src) in enumerate(((A2, bank(0, 0, 128)), (Wvp, bank(0, 128, 256)), (Wsim, bank(5)))):
                        act.wait_ge(s["folded"], n + 1)
                        nc.scalar.activation(dst[:, :], src, ACT.Copy).then_inc(s["fold_copied"], 1)
                    table_ahead(0)
            self_attention(act, step)
            act.wait_ge(s["ln_var"], 1)
            nc.scalar.activation(rstd[:, :], veps[:, :], ACT.Sqrt).then_inc(s["ln_std"], 1)

            def ctx_copies(p, par):
                for g in range(NG):
                    act.wait_ge(s["cT_psum1"], NG * p + (g + 1))
                    nc.scalar.activation(ctxT[par][:, 1, g, :], bank(T_BANKS[g][1], 0, TG * ROWS), ACT.Copy).then_inc(s["cT_a"], 1)

            def prob_copies(p):
                for g in (0, 2):
                    act.wait_ge(s["p2T_psum"], NG * p + (g + 1))
                    nc.scalar.activation(prob2T[0:ROWS, g * TG:(g + 1) * TG, :],
                                         bank(P_BANKS[g])[0:ROWS, :].rearrange("p (t n) -> p t n", t=TG),
                                         ACT.Copy).then_inc(s["p2T_a"], 1)

            def exps(p, par):
                act.wait_ge(s["m2_ready"], p + 1)
                nc.scalar.activation(prob2[par].rearrange("p (g m) -> p g m", g=NG), PS[:, 0:NG, 0:TG * ROWS], ACT.Exp,
                                     bias=nb2[:, 0:1], scale=0.25, accum_out=sum2[:, par:par + 1]).then_inc(s["p2_ready"], 1)

            def out_copy(p):
                act.wait_ge(s["o2T_psum"], p + 1)
                nc.scalar.activation(oT, bank(7, 128, 256), ACT.Copy).then_inc(s["oT_ready"], 1)

            ctx_copies(0, 0)
            for g in range(5):
                if g < 4:
                    act.wait_ge(s["t_psum"], g + 1)
                    nc.scalar.activation(xl2T[:, g * BANK:(g + 1) * BANK], bank(g % 2), ACT.Copy).then_inc(s["t_copied"], 1)
                if g:
                    act.wait_ge(s["q2_psum"], g)
                    nc.scalar.activation(q2T[:, (g - 1) * BANK:g * BANK], bank(Q_BANKS[(g - 1) % 2]), ACT.Copy).then_inc(s["q2_copied"], 1)
            exps(0, 0)
            ctx_copies(1, 1)
            prob_copies(0)
            exps(1, 1)

            def step(p, par):
                out_copy(p - 1)
                ctx_copies(p + 1, 1 - par)
                prob_copies(p)
                exps(p + 1, 1 - par)
            with act.Fori(0, 3) as i:
                for j in range(4):
                    step(4 * i + (j + 1), (j + 1) % 2)
            step(13, 1)
            step(14, 0)
            table_ahead(1)
            out_copy(14)
            prob_copies(15)
            out_copy(15)
            act.wait_ge(s["ln_var"], 2)
            nc.scalar.activation(rstd[:, :], veps[:, :], ACT.Sqrt).then_inc(s["ln_std"], 1)
            for n, dst in enumerate((x2T, xlT)):
                for g in range(4):
                    act.wait_ge(s["t_psum"], 4 * n + g + 5)
                    nc.scalar.activation(dst[:, g * 448:(g + 1) * 448].rearrange("p (a t) -> p a t", t=T),
                                         bank(4 * n + g).rearrange("p (a t) -> p a t", t=TP)[:, :, 0:T], ACT.Copy).then_inc(s["t_copied"], 1)
            act.wait_ge(s["bn_var"], 1)
            nc.scalar.activation(bsc[:, 1:2], bsc[:, 0:1], ACT.Sqrt).then_inc(s["bn_std"], 1)
            act.wait_ge(s["bn_ready"], 1)

            def normed(i, t):
                act.wait_ge(s["sim_psum"], 2 * i + (t + 1))
                nc.scalar.activation(xbn[:, t, :], xlT[:, bass.ds(i * 2 * TILE + t * TILE, TILE)], ACT.Identity,
                                     scale=bsc[:, 2:3], bias=bsc[:, 3:4]).then_inc(s["xbn_ready"], 1)

            def weights(i):
                for t in range(2):
                    act.wait_ge(s["best_ready"], 2 * i + (t + 1))
                    nc.scalar.activation(weight[:, t, :].rearrange("p (h k) -> p h k", h=NH), best[:, t], ACT.Sigmoid).then_inc(s["weight_ready"], 1)

            def rows(i):
                act.wait_ge(s["out_psum"], i + 1)
                act.wait_ge(s["out_done"], 16 * i + 16)
                nc.scalar.activation(res[:, :, :], bank(7, 0, 256).rearrange("p (t c) -> p t c", t=2), ACT.Copy).then_inc(s["res_ready"], 1)

            def gelus(i):
                for r in range(V // 2):
                    act.wait_ge(s["h_psum"], (V // 2) * i + (r + 1))
                    nc.scalar.activation(gelu[:, 2 * r:2 * r + 2, bass.ds(i * 2 * TILE, 2 * TILE)],
                                         bank(6 + r % 2).rearrange("p (v n) -> p v n", v=2), ACT.Gelu).then_inc(s["h_done"], 1)

            for t in range(2):
                normed(0, t)
            gelus(0)
            for t in range(2):
                normed(1, t)
            weights(0)
            with act.Fori(1, DUOS - 1) as i:
                gelus(i)
                for t in range(2):
                    normed(i + 1, t)
                weights(i)
                rows(i - 1)
            gelus(DUOS - 1)
            weights(DUOS - 1)
            rows(DUOS - 2)
            rows(DUOS - 1)

        @block.vector
        def _(dve):
            ch = Chain(dve, s["dve"])

            def variances(done):
                ch.wait()
                for p in range(PAIRS):
                    ch.did(nc.vector.bn_aggr(mv[:, p, :], stats[:, p, :]))
                ch.wait()
                nc.vector.tensor_scalar_add(veps[:, :], mv[:, :, 1], LN_EPS).then_inc(s[done], 1)

            def pair_stats(src, p):
                ch.did(nc.vector.bn_stats(stats[:, bass.ds(p, 1), :].rearrange("p o c -> p (o c)"), src[:, bass.ds(p, 1), :].rearrange("p o c -> p (o c)")))

            def layer_norm(src):
                ch.did(nc.vector.reciprocal(rstd[:, :], rstd[:, :]))
                ch.wait()
                for p in range(PAIRS):
                    last = nc.vector.tensor_scalar(xn_[:, p, :], src[:, p, :], mv[:, p, 0:1], rstd[:, p:p + 1], ALU.subtract, ALU.mult)
                    if p % 4 == 3:
                        last.then_inc(s["ln_done"], 1)
                    else:
                        last.then_inc(s["dve"], 1)
                        ch.n += 1

            ch.did(nc.vector.memset(x0[96:128, :, :], 0.0))
            ch.wait()
            dve.sem_inc(s["pads_zero"], 1)
            dve.wait_ge(s["pads_zero"], 2)
            dve.wait_ge(s["x_in"], 32)
            for p in range(PAIRS):
                ch.did(nc.vector.bn_stats(stats[:, p, :], x0[:, p, :]))
            variances("ln1_var")
            dve.wait_ge(s["ln1_std"], 1)
            ch.did(nc.vector.reciprocal(rstd[:, :], rstd[:, :]))
            ch.wait()
            dve.wait_ge(s["ka_in"], 16)

            def normed(p, par):
                nc.vector.tensor_scalar(xc[par], x0[:, bass.ds(p, 1), :].rearrange("p o c -> p (o c)"), mv[:, bass.ds(p, 1), 0],
                                        rstd[:, bass.ds(p, 1)], ALU.subtract, ALU.mult).then_inc(s["xc_ready"], 1)

            def rotate(p, par):
                dve.wait_ge(s["qk_psum"], p + 1)
                if after(p, 1):
                    dve.wait_ge(s["rot_q_ready"], p)
                nc.vector.tensor_tensor(rope.rearrange("p (t r n) -> p t r n", t=2, r=2), bank(0).rearrange("p (t r n) -> p t r n", t=2, r=2),
                                        KA[:, ca["cos"][0]:ca["sin"][1]].rearrange("p (t o n) -> p t o n", t=2, o=1).to_broadcast([128, 2, 2, 128]),
                                        ALU.mult).then_inc(s["rope_ready"], 1)
                dve.wait_ge(s["rope_ready"], p + 1)
                if after(p, 1):
                    dve.wait_ge(s["kx_ready"], p)
                ch.did(nc.vector.tensor_tensor(rot_k, rope[:, 128:256], rope[:, 384:512], ALU.add))
                ch.wait()
                nc.vector.tensor_tensor(kx[par], rot_k.rearrange("p (o n) -> p o n", o=1).to_broadcast([128, 4, 128]),
                                        wa("slot").rearrange("p (g o) -> p g o", o=1).to_broadcast([128, 4, 128]), ALU.mult).then_inc(s["kx_ready"], 1)

            def softmax(p, par):
                dve.wait_ge(s["s1_psum"], p + 1)
                S = PS[:, 1:3, :].rearrange("p b (h k) -> p (b h) k", k=TP)[:, :, 0:T]
                ch.did(nc.vector.tensor_reduce(neg1[:, :], S, AX.X, ALU.max, negate=True))
                ch.wait()
                nc.vector.tensor_tensor(prob1[par][:, :, 0:T], S, neg1[:, :].rearrange("p (h o) -> p h o", o=1).to_broadcast([128, HEADS, T]),
                                        ALU.add).then_inc(s["s1_read"], 1)

            def normalise1(p):
                dve.wait_ge(s["o1_psum"], p + 1)
                o = bank(6, 0, HEADS // 2 * VW).rearrange("p (h d) -> p h d", d=VW)
                ch.did(nc.vector.reciprocal(inv1[:, :].rearrange("p (h a) -> p h a", a=2), o[:, :, 2 * HD:VW]))
                ch.wait()
                nc.vector.tensor_tensor(att.rearrange("p (h a d) -> p h a d", a=2, d=HD), o[:, :, 0:2 * HD].rearrange("p h (a d) -> p h a d", a=2),
                                        inv1[:, :].rearrange("p (h a o) -> p h a o", a=2, o=1).to_broadcast([128, HEADS // 2, 2, HD]),
                                        ALU.mult).then_inc(s["att_ready"], 1)

            def residual1(p):
                dve.wait_ge(s["y1_psum"], p + 1)
                dve.wait_ge(s["bias_added"], p + 1)
                nc.vector.tensor_tensor(x1[:, bass.ds(p, 1), :], bank(7, 128, 256).rearrange("p (o n) -> p o n", o=1),
                                        x1[:, bass.ds(p, 1), :], ALU.add).then_inc(s["x1_done"], 1)
                dve.wait_ge(s["x1_done"], p + 1)
                pair_stats(x1, p)

            def step(p, par):
                if within(p - 2):
                    normalise1(p - 2)
                if within(p + 1):
                    rotate(p + 1, 1 - par)
                if within(p + 3):
                    normed(p + 3, 1 - par)
                if within(p):
                    softmax(p, par)
                if within(p - 2):
                    residual1(p - 2)
            self_attention(dve, step, ch, 2 * 4)
            variances("ln_var")

            def ctx_copies(p, par):
                for g in range(NG):
                    dve.wait_ge(s["cT_psum0"], NG * p + (g + 1))
                    nc.vector.tensor_copy(ctxT[par][:, 0, g, :], bank(T_BANKS[g][0], 0, TG * ROWS)).then_inc(s["cT_d"], 1)

            def maximum(p):
                dve.wait_ge(s["s2_psum"], p + 1)
                ch.did(nc.vector.tensor_reduce(max2[:, :], PS[:, 0:NG, 0:TG * ROWS], AX.XY, ALU.max))
                ch.wait()
                nc.vector.tensor_scalar_mul(nb2[:, :], max2[:, :], -0.25).then_inc(s["m2_ready"], 1)

            def prob_copy(p, par):
                dve.wait_ge(s["p2_ready"], p + 1)
                nc.vector.reciprocal(inv2[:, par:par + 1], sum2[:, par:par + 1]).then_inc(s["dve"], 1)
                ch.n += 1
                dve.wait_ge(s["p2T_psum"], NG * p + 2)
                nc.vector.tensor_copy(prob2T[0:ROWS, TG:2 * TG, :],
                                      bank(P_BANKS[1])[0:ROWS, :].rearrange("p (t n) -> p t n", t=TG)).then_inc(s["p2T_d"], 1)

            def residual(p, par):
                dve.wait_ge(s["y2_psum"], p + 1)
                nc.vector.tensor_tensor(x2[:, bass.ds(p, 1), :], bank(7, 256, 384).rearrange("p (o n) -> p o n", o=1),
                                        x1[:, bass.ds(p, 1), :], ALU.add).then_inc(s["x2_done"], 1)
                dve.wait_ge(s["x2_done"], p + 2)
                pair_stats(x2, p)

            def normalise(p, par):
                dve.wait_ge(s["o2_psum"], p + 1)
                nc.vector.tensor_scalar(o2, bank(7, 0, 128), inv2[:, par:par + 1], None, ALU.mult).then_inc(s["o2_ready"], 1)

            ctx_copies(0, 0)
            dve.wait_ge(s["ln_std"], 1)
            layer_norm(x1)
            dve.wait_ge(s["ln_done"], 4)
            ch.did(nc.vector.tensor_tensor(x1, x1, wa("bias2").rearrange("p (o c) -> p o c", o=1).to_broadcast([128, PAIRS, C]), ALU.add))
            ch.wait()
            dve.sem_inc(s["x2_done"], 1)
            maximum(0)
            ctx_copies(1, 1)
            prob_copy(0, 0)
            maximum(1)

            def step(p, par):
                normalise(p - 1, 1 - par)
                ctx_copies(p + 1, 1 - par)
                residual(p - 1, 1 - par)
                prob_copy(p, par)
                maximum(p + 1)
            with dve.Fori(0, 3) as i:
                ch.enter(i, 4 * 3)
                for j in range(4):
                    step(4 * i + (j + 1), (j + 1) % 2)
            ch.leave(3)
            step(13, 1)
            step(14, 0)
            normalise(14, 0)
            residual(14, 0)
            prob_copy(15, 1)
            normalise(15, 1)
            residual(15, 1)

            dve.wait_ge(s["x2_done"], PAIRS + 1)
            variances("ln_var")
            dve.wait_ge(s["ln_std"], 2)
            layer_norm(x2)
            for g in range(4):
                dve.wait_ge(s["t_copied"], 8 + g + 1)
                ch.did(nc.vector.bn_stats(bst[:, g, :], xlT[:, g * 448:(g + 1) * 448]))
            ch.wait()
            ch.did(nc.vector.bn_aggr(bmv[:, :], bst[:, :, :].rearrange("p a b -> p (a b)")))
            ch.wait()
            nc.vector.tensor_scalar_add(bsc[:, 0:1], bmv[:, 1:2], BN_EPS).then_inc(s["bn_var"], 1)
            dve.wait_ge(s["bn_std"], 1)
            ch.did(nc.vector.reciprocal(bsc[:, 0:1], bsc[:, 1:2]))
            ch.wait()
            ch.did(nc.vector.tensor_tensor(bsc[:, 2:3], bsc[:, 0:1], wa("gamma"), ALU.mult))
            ch.wait()
            ch.did(nc.vector.tensor_tensor(bsc[:, 0:1], bmv[:, 0:1], bsc[:, 2:3], ALU.mult))
            ch.wait()
            nc.vector.tensor_tensor(bsc[:, 3:4], wa("beta"), bsc[:, 0:1], ALU.subtract).then_inc(s["bn_ready"], 1)
            dve.sem_inc(s["sim_read"], 2)

            def best_keys(i, t):
                dve.wait_ge(s["sim_psum"], 2 * i + (2 + t + 1))
                dve.sem_inc(s["apart"], 1)
                v_t, i_t = val[:, t], idx[:, t]
                sim = bank(4 + t).rearrange("p (a h k) -> p a h k", a=2, h=NH)
                for a in range(2):
                    for h in range(NH):
                        ch.did(nc.vector.max(v_t[:, a, h, :], sim[:, a, h, :]))
                ch.wait_apart(s["apart"])
                for a in range(2):
                    for h in range(NH):
                        ch.did(nc.vector.max_index(i_t[:, a, h, :], v_t[:, a, h, :], sim[:, a, h, :]))
                for a0, na_, nb_, at in SPANS:
                    ch.did(nc.vector.tensor_tensor(
                        cand[:, t, :, at:at + na_ * nb_].rearrange("p h (a b) -> p h a b", b=nb_),
                        v_t[:, 0, :, a0:a0 + na_].rearrange("p h (a o) -> p h a o", o=1).to_broadcast([128, NH, na_, nb_]),
                        v_t[:, 1, :, 0:nb_].rearrange("p h (o b) -> p h o b", o=1).to_broadcast([128, NH, na_, nb_]), ALU.add))
                ch.wait()
                dve.sem_inc(s["sim_read"], 1)
                dve.sem_inc(s["index_ready"], 1)
                for h in range(NH):
                    ch.did(nc.vector.max(best[:, t, h, :], cand[:, t, h, :]))
                ch.wait_apart(s["apart"])
                dve.sem_inc(s["best_ready"], 1)
                for h in range(NH):
                    ch.did(nc.vector.max_index(pos[:, t, h, :], best[:, t, h, :], cand[:, t, h, :]))
                ch.wait()
                nc.vector.tensor_tensor(
                    hit[:, :, t, :], pos[:, t].rearrange("p (o h) k -> p o (h k)", o=1).to_broadcast([128, NCAND, HK]),
                    iota_c[:, :, :], ALU.is_equal).then_inc(s["hit_ready"], 1)

            def picks(i, first=False):
                dve.wait_ge(s["ew_psum"], i + 1)
                ch.did(nc.vector.tensor_copy(eT[:, :], bank(6, 0, 128)))
                ch.did(nc.vector.tensor_scalar_mul(w_hi[:, :], bank(6, 128, 256), W_UP))
                ch.wait()
                ch.did(nc.vector.scalar_tensor_tensor(w_lo[:, :], bank(6, 128, 256), W_UP, w_hi[:, :], ALU.mult, ALU.subtract))
                ch.did(nc.vector.tensor_single_scalar(eu[:, 0, :], eT[:, :], EXPERTS - V, op=ALU.bitwise_and))
                ch.did(nc.vector.tensor_single_scalar(ev[:, :], eT[:, :], V - 1, op=ALU.bitwise_and))
                ch.wait()
                dve.sem_inc(s["ew_read"], 1)
                ch.did(nc.vector.tensor_single_scalar(eu[:, 1, :], eu[:, 0, :], EXPERTS // 2, op=ALU.bitwise_xor))
                if not first:
                    dve.wait_ge(s["mix_psum"], i)
                ch.did(nc.vector.tensor_tensor(pick_v[:, :, :], ev[:, :].rearrange("p (o n) -> p o n", o=1).to_broadcast([128, V, TILE]),
                                               iota_v[:, :, :], ALU.is_equal))
                ch.wait()
                ch.did(nc.vector.tensor_tensor(pick_u.rearrange("p (a u) n -> p a u n", a=2),
                                               eu[:, :, :].rearrange("p a (o n) -> p a o n", o=1).to_broadcast([128, 2, U // 2, TILE]),
                                               iota_u.rearrange("p (o u) n -> p o u n", o=1).to_broadcast([128, 2, U // 2, TILE]), ALU.is_equal))
                ch.wait()
                for t in range(2):
                    for dst, w in ((b_hi, w_hi), (b_lo, w_lo)):
                        r = slice(t * HK, (t + 1) * HK)
                        ch.did(nc.vector.tensor_tensor(dst[r, t * V:(t + 1) * V, :], pick_v[r, :, :],
                                                       w[r, :].rearrange("p (o n) -> p o n", o=1).to_broadcast([HK, V, TILE]), ALU.mult))
                ch.wait()
                dve.sem_inc(s["picks"], 1)

            def mix(i):
                dve.wait_ge(s["mix_psum"], i + 1)
                dve.wait_ge(s["h_done"], (V // 2) * (i + 1))
                for t in range(2):
                    for b in range(4):
                        src = bank(b).rearrange("p (n t v) -> p t v n", t=2, v=V)
                        ch.did(nc.vector.scalar_tensor_tensor(
                            act_w[:, t, :, b * 32:(b + 1) * 32], src[:, t], 1.0 / W_UP,
                            gelu[:, :, bass.ds(i * 2 * TILE + t * TILE + b * 32, 32)], ALU.mult, ALU.mult))
                ch.wait()
                dve.sem_inc(s["mixed"], 1)

            dve.wait_ge(s["iota_done"], 1)

            for t in range(2):
                best_keys(0, t)
            picks(0, True)
            with dve.Fori(0, DUOS - 1) as i:
                ch.enter(i, 2 * (16 + 16 + 4 + 8 + 8) + 6 + 2 + 4 + 8)
                for t in range(2):
                    best_keys(i + 1, t)
                mix(i)
                picks(i + 1)
            ch.leave(DUOS - 1)
            mix(DUOS - 1)

        @block.tensor
        def _(pe):
            mm = nc.tensor.matmul
            one = dict(start=True, stop=True)
            pe.wait_ge(s["ka_in"], 16)

            def projections(p, par):
                pe.wait_ge(s["xcT_ready"], p + 1)
                if after(p, 1):
                    pe.wait_ge(s["rope_ready"], p)
                for n, w in enumerate(("wq", "wk", "wqs", "wks")):
                    last = mm(bank(0, n * 128, n * 128 + 128), wa(w), xcT[par], **one)
                last.then_inc(s["qk_psum"], 1)

            def turn1(p):
                pe.wait_ge(s["att_ready"], p + 1)
                if after(p, 1):
                    pe.wait_ge(s["x1_done"], p)
                nc.tensor.transpose(bank(7, 0, 128), att, ident).then_inc(s["attT_psum"], 1)

            def values(p, par):
                if after(p, 1):
                    pe.wait_ge(s["vx_ready"], 2 * p)
                for b in range(2):
                    for a in range(2):
                        last = mm(bank(5, b * 64, b * 64 + 64)[a * TP:(a + 1) * TP, :], xcT[par][:, b * TP:(b + 1) * TP],
                                  wa("wv")[:, a * 64:a * 64 + 64], **one)
                last.then_inc(s["v_psum"], 1)

            def turn_rows(p, par):
                pe.wait_ge(s["xc_ready"], p + 1)
                if after(p, 5):
                    pe.wait_ge(s["att_ready"], p - 3)
                nc.tensor.transpose(bank(6, 256, 384), xc[par], ident).then_inc(s["xcT_psum"], 1)

            def scores1(p, par):
                pe.wait_ge(s["qx_ready"], p + 1)
                pe.wait_ge(s["kx_ready"], p + 1)
                if after(p, 1):
                    pe.wait_ge(s["s1_read"], p)
                for g in range(4):
                    for b in range(2):
                        o = PS[b * TP:(b + 1) * TP, 1 + g // 2, (g % 2) * 256:(g % 2) * 256 + 256].rearrange("p (h k) -> p h k", k=TP)[:, :, 0:T]
                        last = mm(o, qx[par][:, g, b * TP:(b + 1) * TP], kx[par][:, :, b * TP:b * TP + T], **one)
                last.then_inc(s["s1_psum"], 1)

            def project1(p):
                pe.wait_ge(s["attT_ready"], p + 1)
                mm(bank(7, 128, 256), attT, wa("wproj"), **one).then_inc(s["y1_psum"], 1)

            def prob_transposes(p, par):
                pe.wait_ge(s["p1_ready"], p + 1)
                for h in range(HEADS // 2):
                    last = nc.tensor.transpose(bank(3 + h // 4, (h % 4) * 128, (h % 4) * 128 + 128),
                                               prob1[par][:, 2 * h:2 * h + 2, :].rearrange("p h k -> p (h k)"), ident)
                    if h % 4 == 3:
                        last.then_inc(s["p1T_psum"], 1)

            def products1(p, par):
                pe.wait_ge(s["xcT_ready"], min(p + 4, PAIRS) if isinstance(p, int) else p + 4)
                pe.wait_ge(s["vx_ready"], 2 * p + 2)
                for h in range(HEADS // 2):
                    if h % 4 == 0:
                        pe.wait_ge(s["p1T_ready"], 2 * p + (1 + h // 4))
                    for b in range(2):
                        last = mm(bank(6, h * VW, (h + 1) * VW)[b * TP:(b + 1) * TP, :],
                                  prob1T[:, h, b * TP:(b + 1) * TP], vx[par][:, b, h, :], **one)
                last.then_inc(s["o1_psum"], 1)

            def fold():
                pe.wait_ge(s["rope_ready"], PAIRS)
                mm(bank(0, 0, 128), wa("xwq"), wa("xwk"), **one).then_inc(s["folded"], 1)
                mm(bank(0, 128, 256), wa("xwv"), wa("xproj"), **one).then_inc(s["folded"], 1)
                pe.wait_ge(s["kb_in"], 32)
                pe.wait_ge(s["vx_ready"], 2 * PAIRS)
                for n in range(2 * NH):
                    last = mm(bank(5, n * NK, (n + 1) * NK), fwq[:, n * C:(n + 1) * C], wb("keys")[:, n * NK:(n + 1) * NK], **one)
                last.then_inc(s["folded"], 1)

            def step(p, par):
                if isinstance(p, int) and p == PAIRS:
                    fold()
                if within(p + 1):
                    projections(p + 1, 1 - par)
                if within(p - 2):
                    turn1(p - 2)
                if within(p):
                    values(p, par)
                if within(p + 2):
                    turn_rows(p + 2, par)
                if within(p):
                    scores1(p, par)
                if within(p - 2):
                    project1(p - 2)
                if within(p - 1):
                    prob_transposes(p - 1, 1 - par)
                    products1(p - 1, 1 - par)
            self_attention(pe, step)

            def ctx_transposes(p, slot, groups=range(NG)):
                for g in groups:
                    for b in range(2):
                        if g == 2:
                            pe.wait_ge(s["cT_d" if b == 0 else "cT_a"], NG * p + 1)
                        for k in range(TG):
                            last = nc.tensor.transpose(bank(T_BANKS[g][b], k * ROWS, (k + 1) * ROWS), ring[slot][0:ROWS, b, g * TG + k, :],
                                                       ident[0:ROWS, 0:ROWS])
                        last.then_inc(s[f"cT_psum{b}"], 1)

            def scores(p, par):
                pe.wait_ge(s["q2_ready"], p + 1)
                for g in range(NG):
                    pe.wait_ge(s["cT_d"], NG * p + (g + 1))
                    pe.wait_ge(s["cT_a"], NG * p + (g + 1))
                    for b in range(2):
                        last = mm(PS[b * TP:(b + 1) * TP, g, 0:TG * ROWS], q2[par][:, b * TP:(b + 1) * TP], ctxT[par][:, b, g, :], **one)
                last.then_inc(s["s2_psum"], 1)

            def products(p, par, slot):
                pe.wait_ge(s["p2_ready"], p + 1)
                for g in range(NG):
                    for k in range(TG):
                        t = g * TG + k
                        last = nc.tensor.transpose(bank(P_BANKS[g], k * 128, k * 128 + 128)[0:ROWS, :],
                                                   prob2[par][:, t * ROWS:(t + 1) * ROWS], ident)
                    last.then_inc(s["p2T_psum"], 1)
                for g in range(NG):
                    if g == 1:
                        pe.wait_ge(s["p2T_d"], p + 1)
                    else:
                        pe.wait_ge(s["p2T_a"], 2 * p + (1 if g == 0 else 2))
                    for t in range(g * TG, (g + 1) * TG):
                        for b in range(2):
                            last = mm(bank(7, 0, 128)[b * TP:(b + 1) * TP, :], prob2T[0:ROWS, t, b * TP:(b + 1) * TP],
                                      ring[slot][0:ROWS, b, t, :], start=t == 0, stop=t == NT - 1)
                last.then_inc(s["o2_psum"], 1)

            def turn(p):
                pe.wait_ge(s["o2_ready"], p + 1)
                nc.tensor.transpose(bank(7, 128, 256), o2, ident).then_inc(s["o2T_psum"], 1)

            def project(p):
                pe.wait_ge(s["oT_ready"], p + 1)
                mm(bank(7, 256, 384), oT, Wvp[:, :], **one).then_inc(s["y2_psum"], 1)

            def arrived(slot, use):
                pe.wait_ge(s[f"ctx{slot}"], 32 * use)

            pe.wait_ge(s["fold_copied"], 3)
            arrived(0, 1)
            ctx_transposes(0, 0)
            pe.wait_ge(s["x1_done"], PAIRS)
            for g in range(5):
                if g < 4:
                    pe.wait_ge(s["ln_done"], g + 1)
                    if g >= 2:
                        pe.wait_ge(s["t_copied"], g - 1)
                    for a in range(4):
                        last = nc.tensor.transpose(bank(g % 2, a * 128, a * 128 + 128), xn_[:, 4 * g + a, :], ident)
                    last.then_inc(s["t_psum"], 1)
                if g:
                    pe.wait_ge(s["t_copied"], g)
                    if g >= 3:
                        pe.wait_ge(s["q2_copied"], g - 2)
                    mm(bank(Q_BANKS[(g - 1) % 2]), A2[:, :], xl2T[:, (g - 1) * BANK:g * BANK], **one).then_inc(s["q2_psum"], 1)
            pe.wait_ge(s["q2_copied"], 4)
            scores(0, 0)
            arrived(1, 1)
            ctx_transposes(1, 1)
            scores(1, 1)
            products(0, 0, 0)

            def step(p, par, slot, use):
                arrived((slot + 1) % RING, use)
                ctx_transposes(p + 1, (slot + 1) % RING, (0,))
                turn(p - 1)
                ctx_transposes(p + 1, (slot + 1) % RING, (1, 2))
                project(p - 1)
                scores(p + 1, 1 - par)
                pe.wait_ge(s["x2_done"], p + 1)
                products(p, par, slot)
            with pe.Fori(0, 3) as i:
                for j in range(4):
                    step(4 * i + (j + 1), (j + 1) % 2, (j + 1) % RING, i + (1 + (j + 2) // RING))
            step(13, 1, 1, 4)
            step(14, 0, 2, 4)
            turn(14)
            project(14)
            pe.wait_ge(s["x2_done"], PAIRS)
            products(15, 1, 3)
            turn(15)
            project(15)

            pe.wait_ge(s["x2_done"], PAIRS + 1)
            for n, src in enumerate((x2, xn_)):
                for g in range(4):
                    if n:
                        pe.wait_ge(s["ln_done"], 4 + g + 1)
                    for a in range(4):
                        last = nc.tensor.transpose(bank(4 * n + g, a * 128, a * 128 + 128), src[:, 4 * g + a, :], ident)
                    last.then_inc(s["t_psum"], 1)
            pe.wait_ge(s["t_copied"], 12)
            pe.sem_inc(s["sim_psum"], 2)

            def hidden(i, first=False):
                for r in range(V // 2):
                    if r == 0:
                        if not first:
                            pe.wait_ge(s["ew_read"], i)
                    elif r == 1:
                        if not first:
                            pe.wait_ge(s["res_ready"], i)
                    else:
                        pe.wait_ge(s["h_done"], (V // 2) * i + (r - 1))
                    for k in range(2):
                        v = 2 * r + k
                        last = mm(bank(6 + r % 2, k * 256, k * 256 + 256), wb("down")[:, v * U:(v + 1) * U],
                                  xlT[:, bass.ds(i * 2 * TILE, 2 * TILE)], **one)
                    last.then_inc(s["h_psum"], 1)

            def key_scores(i):
                for t in range(2):
                    pe.wait_ge(s["xbn_ready"], 2 * i + (t + 1))
                    pe.wait_ge(s["sim_read"], 2 * i + (t + 1))
                    mm(bank(4 + t), xbn[:, t, :], Wsim[:, :], **one).then_inc(s["sim_psum"], 1)

            def expert_transposes(i):
                pe.wait_ge(s["expert_ready"], 2 * i + 2)
                pe.wait_ge(s["h_done"], (V // 2) * (i + 1) - 1)
                for n in range(NCAND):
                    mm(bank(6, 0, 128), hit[:, n, :, :].rearrange("p t k -> p (t k)"), ident16[:, :], start=n == 0, stop=n == NCAND - 1)
                pe.wait_ge(s["weight_ready"], 2 * i + 2)
                nc.tensor.transpose(bank(6, 128, 256), weight[:, :, :].rearrange("p t k -> p (t k)"), ident).then_inc(s["ew_psum"], 1)

            def spread(i):
                pe.wait_ge(s["picks"], i + 1)
                for n in range(TILE):
                    o = bank(n // 32, (n % 32) * 16, (n % 32) * 16 + 16)
                    mm(o, pick_u[:, :, n], b_hi[:, :, n], start=True, stop=False)
                    last = mm(o, pick_u[:, :, n], b_lo[:, :, n], start=False, stop=True)
                last.then_inc(s["mix_psum"], 1)

            def gather(i, n_hidden):
                pe.wait_ge(s["mixed"], i + 1)
                pe.wait_ge(s["x2s_ready"], i + 1)
                pe.wait_ge(s["h_done"], (V // 2) * n_hidden)
                pe.wait_ge(s["res_ready"], i + 1)
                for t in range(2):
                    o = bank(7, t * 128, t * 128 + 128)
                    mm(o, x2s[:, t, :], ident, start=True, stop=False)
                    for v in range(V):
                        last = mm(o, act_w[:, t, v, :], wb("up")[:, v * C:(v + 1) * C], start=False, stop=v == V - 1)
                last.then_inc(s["out_psum"], 1)

            key_scores(0)
            hidden(0, True)
            key_scores(1)
            expert_transposes(0)
            spread(0)
            with pe.Fori(1, DUOS - 1) as i:
                hidden(i)
                key_scores(i + 1)
                expert_transposes(i)
                gather(i - 1, i + 1)
                spread(i)
            hidden(DUOS - 1)
            expert_transposes(DUOS - 1)
            gather(DUOS - 2, DUOS)
            spread(DUOS - 1)
            gather(DUOS - 1, DUOS)


def constants():
    import numpy as np
    p = np.arange(128)
    inv = (1.0 / 10000.0 ** (np.arange(0, HD, 2, dtype=np.float32) / np.float32(HD))).astype(np.float32)
    ang = np.arange(T, dtype=np.float32)[None, :] * inv[(p % HD) // 2][:, None]
    cos = np.zeros((128, 2, TP), np.float32)
    sin = np.zeros((128, 2, TP), np.float32)
    cos[:, :, :T] = np.cos(ang)[:, None, :]
    sin[:, :, :T] = np.where(p % 2 == 0, -1.0, 1.0)[:, None, None] * np.sin(ang)[:, None, :]
    four = np.arange(4)
    return {
        "ident": np.eye(128, dtype=np.float32),
        "cos": cos.reshape(128, 2 * TP).astype(np.float32), "sin": sin.reshape(128, 2 * TP).astype(np.float32),
        "slot": ((p // HD % 4)[:, None] == four).astype(np.float32),
        "group": ((p // 32)[:, None] == four).astype(np.float32),
    }


def kernel(**inputs):
    import numpy as np
    import concourse.bacc as bacc
    from concourse.bass_utils import run_bass_kernel_spmd

    a = {k: np.asarray(v) for k, v in inputs.items()}
    qkv = a["L0_attn_w_qkv"]
    swapped = qkv.reshape(3 * C // 2, 2, C)[:, ::-1].reshape(3 * C, C)
    row = lambda b: np.broadcast_to(b[None, :], (128, C))
    cols = {
        "wq": qkv[:C].T, "wqs": swapped[:C].T, "wk": qkv[C:2 * C].T, "wks": swapped[C:2 * C].T,
        "wv": qkv[2 * C:].reshape(HEADS // 2, 2, HD, C).transpose(1, 0, 2, 3).reshape(C, C).T,
        "wproj": a["L0_attn_w_proj"].T,
        "xwq": a["L0_xattn_wq"].T, "xwk": a["L0_xattn_wk"].T, "xwv": a["L0_xattn_wv"].T, "xproj": a["L0_xattn_w_proj"],
        "bias1": row(a["L0_attn_b_proj"]), "bias2": row(a["L0_xattn_b_proj"]),
        "gamma": a["L0_ffn_bn_gamma"][:, None], "beta": a["L0_ffn_bn_beta"][:, None],
        "keys": a["L0_ffn_keys_p"].transpose(3, 2, 0, 1).reshape(C, -1),
        "down": a["L0_ffn_down"][:EXPERTS].reshape(U, V, C).transpose(2, 1, 0).reshape(C, -1),
        "up": a["L0_ffn_up"][:EXPERTS].reshape(U, V * C),
        **constants(),
    }
    arrays = {
        "x": np.ascontiguousarray(a["x"]), "ctx": np.ascontiguousarray(a["ctx_1024"]),
        "pack_a": np.ascontiguousarray(np.concatenate([cols[n] for n, _ in PACK_A], axis=1)),
        "pack_b": np.ascontiguousarray(np.concatenate([cols[n] for n, _ in PACK_B], axis=1)),
        "pack_q": np.ascontiguousarray(a["L0_ffn_w_q"].reshape(2 * NH, C, C).transpose(1, 0, 2).reshape(C, -1)),
    }
    nc = bacc.Bacc("TRN2", target_bir_lowering=False, num_devices=1)
    args = [nc.dram_tensor(n, v.shape, mybir.dt.from_np(v.dtype), kind="ExternalInput").ap() for n, v in arrays.items()]
    out = nc.dram_tensor("out", (B, T, C), F32, kind="ExternalOutput").ap()
    decoder_block(nc, *args, out)
    r = run_bass_kernel_spmd(nc, [arrays], core_ids=[0])
    return r.results[0]["out"]
```

```python
import concourse.bass as bass
from concourse import mybir
from contextlib import ExitStack

F32 = mybir.dt.float32
F16 = mybir.dt.float16
U16 = mybir.dt.uint16
ALU = mybir.AluOpType
ACT = mybir.ActivationFunctionType
AX = mybir.AxisListType

B, T, C = 32, 56, 128
CTX = 1500
HEADS, HD = 16, 8
NH, NK, TOPK = 8, 32, 8
TP = 64
PAIRS = B // 2
AHEAD = 3
LOOPED = PAIRS - 2 * AHEAD
TOK = B * T
VW = 2 * HD + 2
ROWS = 125
NT = CTX // ROWS
BANK = 512
TG = 4
NG = NT // TG
SPREAD = 112
RING = 4
TILE = 128
DUOS = TOK // (2 * TILE)
EXPERTS = NK * NK
U, V = 128, 8
HK = NH * TOPK
NCAND = 20
SPANS = ((0, 1, 8, 0), (1, 1, 4, 8), (2, 2, 2, 12), (4, 4, 1, 16))
LN_EPS = 1e-5
BN_EPS = 1e-5
W_UP = 16384.0

PACK_A = [("wq", C), ("wqs", C), ("wk", C), ("wks", C), ("wv", C), ("wproj", C),
          ("xwq", C), ("xwk", C), ("xwv", C), ("xproj", C), ("ident", C), ("cos", 2 * TP), ("sin", 2 * TP),
          ("slot", 4), ("group", 4), ("bias1", C), ("bias2", C), ("gamma", 1), ("beta", 1)]
PACK_B = [("keys", 2 * NH * NK), ("down", EXPERTS), ("up", EXPERTS)]


def columns(pack):
    at, out = 0, {}
    for name, n in pack:
        out[name] = (at, at + n)
        at += n
    return out, at


class Chain:

    def __init__(self, eng, sem):
        self.eng, self.sem, self.base, self.n = eng, sem, 0, 0

    def did(self, ins):
        ins.then_inc(self.sem, 1)
        self.n += 1
        return ins

    def wait(self, but=0):
        self.eng.wait_ge(self.sem, self.base + self.n - but)

    def wait_apart(self, stand, but=0):
        self.wait(but)
        self.eng.sem_inc(stand, 1)

    def enter(self, i, per_pass):
        self.start, self.per_pass = self.n, per_pass
        self.base = i * per_pass

    def leave(self, passes):
        assert self.n - self.start == self.per_pass, (self.n - self.start, self.per_pass)
        self.n, self.base = self.start + self.per_pass * passes, 0


def decoder_block(nc, x, zeros, ctx, pack_a, pack_b, pack_q, out):
    ca, na = columns(PACK_A)
    cb, nb = columns(PACK_B)
    with ExitStack() as stack:
        def sb(name, shape, dt=F32):
            return stack.enter_context(nc.sbuf_tensor(name, shape, dt))

        def sem(name):
            return stack.enter_context(nc.semaphore(name))

        KA = sb("KA", [128, na])
        KB = sb("KB", [128, nb])
        def wa(name):
            return KA[:, ca[name][0]:ca[name][1]]
        def wb(name):
            return KB[:, cb[name][0]:cb[name][1]]
        ident = wa("ident")

        XA = sb("XA", [128, 4 * PAIRS * C])
        def xpart(n):
            return XA[:, n * PAIRS * C:(n + 1) * PAIRS * C].rearrange("p (a c) -> p a c", c=C)
        x0 = xpart(0)
        fwq = XA[:, 0:2 * NH * C]
        xl2T = XA[:, PAIRS * C:2 * PAIRS * C]
        x1 = xpart(2)
        q2T = XA[:, 3 * PAIRS * C:4 * PAIRS * C]
        xn_ = sb("xn", [128, PAIRS, C])
        x2 = sb("x2", [128, PAIRS, C])
        x2T = sb("x2T", [128, TOK])
        xlT = sb("xlT", [128, TOK])
        stats = sb("stats", [128, PAIRS, 6])
        mv = sb("mv", [128, PAIRS, 2])
        rstd = sb("rstd", [128, PAIRS])
        veps = sb("veps", [128, PAIRS])
        A2 = sb("A2", [128, C])
        Wvp = sb("Wvp", [128, C])
        Wsim = sb("Wsim", [128, 2 * NH * NK])

        CTXF = 2 * NT * C
        ARENA = RING * CTXF + 2 * CTXF + 2 * CTX + NT * 128 + 1536
        AR = sb("AR", [128, ARENA])
        used = [0]
        def take(n):
            at = used[0]
            used[0] += n
            assert used[0] <= ARENA, (used[0], ARENA)
            return AR[:, at:at + n]
        ring = [take(CTXF).rearrange("p (b t c) -> p b t c", b=2, t=NT) for _ in range(RING)]
        after_ring = used[0]
        ctxT = [take(2 * CTX).rearrange("p (b g m) -> p b g m", b=2, g=NG) for _ in range(2)]
        prob2 = [take(CTX) for _ in range(2)]
        prob2T = take(NT * 128).rearrange("p (t n) -> p t n", t=NT)
        q2 = [take(128) for _ in range(2)]
        o2 = take(128)
        oT = take(128)
        used[0] = after_ring
        xc = [take(C) for _ in range(2)]
        xcT = [take(128) for _ in range(2)]
        rope = take(4 * 128)
        rot_q = take(128)
        rot_k = take(128)
        qx = [take(4 * 128).rearrange("p (g n) -> p g n", g=4) for _ in range(2)]
        kx = [take(4 * 128).rearrange("p (g n) -> p g n", g=4) for _ in range(2)]
        prob1 = [take(HEADS * TP).rearrange("p (h k) -> p h k", h=HEADS) for _ in range(2)]
        prob1T = take(HEADS // 2 * 128).rearrange("p (h n) -> p h n", n=128)
        vx = [take(2 * HEADS // 2 * VW).rearrange("p (b h d) -> p b h d", b=2, d=VW) for _ in range(2)]
        att = take(C)
        attT = take(C)
        used[0] = 0
        gelu = take(V * TOK).rearrange("p (v n) -> p v n", v=V)
        pick_u = take(U * TILE // 2).bitcast(F16).rearrange("p (u n) -> p u n", u=U)
        neg1 = sb("neg1", [128, HEADS])
        inv1 = sb("inv1", [128, HEADS])
        max2 = sb("max2", [128, 1])
        nb2 = sb("nb2", [128, 1])
        sum2 = sb("sum2", [128, 2])
        inv2 = sb("inv2", [128, 2])
        bst = sb("bst", [128, 4, 6])
        bmv = sb("bmv", [128, 2])
        bsc = sb("bsc", [128, 4])
        spare = sb("spare", [128, 2])
        xbn = sb("xbn", [128, 2, TILE])
        x2s = sb("x2s", [128, 2, TILE])
        val = sb("val", [128, 2, 2, NH, TOPK])
        idx = sb("idx", [128, 2, 2, NH, TOPK], U16)
        idf = sb("idf", [128, 2, 2, NH, TOPK])
        cand = sb("cand", [128, 2, NH, NCAND])
        cexp = sb("cexp", [128, NCAND, 2, NH])
        best = sb("best", [128, 2, NH, TOPK])
        pos = sb("pos", [128, 2, NH, TOPK], U16)
        hit = xn_[:, :, :].rearrange("p a c -> p (a c)")[:, 0:NCAND * HK].bitcast(F16).rearrange("p (c t k) -> p c t k", c=NCAND, t=2)
        ident16 = sb("ident16", [128, 128], F16)
        weight = sb("weight", [128, 2, HK])
        eT = sb("eT", [128, TILE], U16)
        eu = sb("eu", [128, TILE], U16)
        eu8 = sb("eu8", [128, V, TILE], U16)
        ev = sb("ev", [128, TILE], U16)
        w_hi = sb("w_hi", [128, TILE], F16)
        w_lo = sb("w_lo", [128, TILE], F16)
        pick_v = sb("pick_v", [128, V, TILE], F16)
        b_hi = sb("b_hi", [128, 2 * V, TILE], F16)
        b_lo = sb("b_lo", [128, 2 * V, TILE], F16)
        act_w = x2[:, :, :].rearrange("p a c -> p (a c)").rearrange("p (t v n) -> p t v n", t=2, v=V)
        iota_v = sb("iota_v", [128, V, TILE], U16)
        iota_c = sb("iota_c", [128, NCAND, HK], U16)
        res = sb("res", [128, 2, C])

        PS = stack.enter_context(nc.psum_tensor("PS", [128, 8, BANK], F32))
        X_BANK = 5
        Q_BANKS = (0, 0, 0, 7)
        T_BANKS = ((3, 4), (5, 6), (3, 4))
        T_BANKS_0 = ((1, 2),) * 3
        P_BANKS = (5, 6, 3)

        TURNS = ((1, 0, 0), (1, 1, 1), (1, 2, 2), (0, 0, 4), (0, 1, 5), (0, 2, 6), (1, 3, 3), (0, 3, 0))

        def bank(n, a=0, b=BANK):
            return PS[:, n, a:b]

        s = {n: sem(n) for n in (
            "pads_in x_in0 x_in1 ka_in kb_in out_done ctx0 ctx1 ctx2 ctx3 "
            "dve pool apart apart_pool zeros_done folded fold_copied "
            "ln1_var ln1_std xc_ready xcT_psum xcT_ready qk_psum rope_ready rot_q_ready kx_ready qx_ready bias_added "
            "s1_psum s1_read v_psum vx_ready p1_ready p1T_psum p1T_ready o1_psum att_ready attT_psum attT_ready "
            "y1_psum x1_done "
            "ln_var ln_std ln_done t_psum t_copied q2_psum q2_copied q2_ready "
            "cT_psum0 cT_psum1 cT_a cT_d s2_psum m2_ready p2_ready p2T_psum p2T_a p2T_d o2_psum o2_ready o2T_psum oT_ready y2_psum x2_done "
            "bn_var bn_std bn_ready h_psum h_done iota_done "
            "xbn_ready sim_psum sim_read best_ready weight_ready index_ready hit_ready expert_ready "
            "x2s_ready ew_psum ew_copied ew_read eu8_ready first_u picks mix_psum bank_spread mix_copied mixed out_psum res_ready").split()}
        block = stack.enter_context(nc.Block())

        @block.sync
        def _(sp):
            sp.sem_inc(s["out_done"], 16)
            rows_out = out.rearrange("b t c -> (b t) c")
            for b in range(2):
                sp.dma_start(x0[b * TP + T:(b + 1) * TP, :, :], zeros).then_inc(s["pads_in"], 16)
            rows_in = x.rearrange("(a b) t c -> b t a c", b=2)

            def load_rows(n):
                half = slice(n * PAIRS // 2, (n + 1) * PAIRS // 2)
                for b in range(2):
                    sp.dma_start(x0[b * TP:b * TP + T, half, :], rows_in[b, :, half, :]).then_inc(s[f"x_in{n}"], 16)
            load_rows(0)
            sp.dma_start(KA[:, :], pack_a).then_inc(s["ka_in"], 16)
            load_rows(1)
            sp.dma_start(KB[:, :], pack_b).then_inc(s["kb_in"], 16)

            def load(p, slot):
                src = ctx[bass.ds(2 * p, 2), :, :].rearrange("b (p t) c -> p b t c", t=NT)
                for a, z in ((0, SPREAD), (SPREAD, ROWS)):
                    sp.dma_start(ring[slot][a:z], src[a:z]).then_inc(s[f"ctx{slot}"], 16)

            for p in range(RING):
                load(p, p)
            sp.wait_ge(s["bias_added"], PAIRS)
            sp.dma_start(fwq, pack_q).then_inc(s["kb_in"], 16)
            with sp.Fori(0, PAIRS // RING - 1) as i:
                for j in range(RING):
                    sp.wait_ge(s["o2_psum"], i * RING + (j + 1))
                    load((i + 1) * RING + j, j)
            with sp.Fori(0, DUOS) as i:
                sp.wait_ge(s["res_ready"], i + 2)
                sp.dma_start(rows_out[bass.ds(i * 2 * TILE, 2 * TILE), :].rearrange("(t p) c -> p t c", p=TILE),
                             res[:, :, :]).then_inc(s["out_done"], 16)
            sp.wait_ge(s["out_done"], 16 * DUOS + 16)

        @block.gpsimd
        def _(pool):
            ch = Chain(pool, s["pool"])
            for n in range(2):
                ch.did(nc.gpsimd.memset(prob1[n][:, :, T:TP], 0.0))
                ch.did(nc.gpsimd.memset(vx[n], 0.0))
            ch.wait()
            for n in range(2):
                ch.did(nc.gpsimd.memset(vx[n][0:TP, :, :, 2 * HD:2 * HD + 1], 1.0))
            ch.wait()
            for n in range(2):
                ch.did(nc.gpsimd.memset(vx[n][TP:128, :, :, 2 * HD + 1:VW], 1.0))
            ch.wait()
            pool.sem_inc(s["zeros_done"], 1)
            pool.wait_ge(s["ka_in"], 16)
            for name in ("pads_in", "x_in0", "x_in1"):
                pool.wait_ge(s[name], 32)

            def rotate(p, par):
                pool.wait_ge(s["rope_ready"], p + 1)
                pool.sem_inc(s["apart_pool"], 1)
                nc.gpsimd.tensor_tensor(rot_q, rope[:, 0:128], rope[:, 256:384], ALU.add).then_inc(s["rot_q_ready"], 1)
                pool.wait_ge(s["rot_q_ready"], p + 1)
                pool.sem_inc(s["apart_pool"], 1)
                nc.gpsimd.tensor_tensor(qx[par], rot_q.rearrange("p (o n) -> p o n", o=1).to_broadcast([128, 4, 128]),
                                        wa("group").rearrange("p (g o) -> p g o", o=1).to_broadcast([128, 4, 128]), ALU.mult).then_inc(s["qx_ready"], 1)
                nc.gpsimd.tensor_tensor(x1[:, bass.ds(p, 1), :], x0[:, bass.ds(p, 1), :],
                                        wa("bias1").rearrange("p (o c) -> p o c", o=1), ALU.add).then_inc(s["bias_added"], 1)
                pool.wait_ge(s["qx_ready"], p + 1)
                pool.sem_inc(s["apart_pool"], 1)
            rotate(0, 0)
            rotate(1, 1)
            with pool.Fori(1, PAIRS // 2) as i:
                for j in range(2):
                    rotate(2 * i + j, j)
            ch.did(nc.gpsimd.memset(b_hi[:, :, :], 0.0))
            ch.did(nc.gpsimd.memset(b_lo[:, :, :], 0.0))
            ch.did(nc.gpsimd.iota(iota_v[:, :, :], pattern=[[1, V], [0, TILE]], base=0, channel_multiplier=0))
            ch.did(nc.gpsimd.iota(iota_c[:, :, :], pattern=[[1, NCAND], [0, HK]], base=0, channel_multiplier=0))
            ch.did(nc.gpsimd.tensor_copy(ident16[:, :], ident))
            ch.wait()
            pool.sem_inc(s["iota_done"], 1)

            pool.wait_ge(s["q2_copied"], 1)
            for p in range(2):
                nc.gpsimd.tensor_copy(q2[p], q2T[:, p * 128:(p + 1) * 128]).then_inc(s["q2_ready"], 1)
            pool.wait_ge(s["q2_copied"], 4)
            with pool.Fori(0, PAIRS // 2 - 1) as i:
                for j in range(2):
                    pool.wait_ge(s["s2_psum"], 2 * i + (j + 1))
                    pool.sem_inc(s["apart_pool"], 1)
                    nc.gpsimd.tensor_copy(q2[j], q2T[:, bass.ds((2 * i + 2 + j) * 128, 128)]).then_inc(s["q2_ready"], 1)
            def experts(i, t):
                pool.wait_ge(s["index_ready"], 2 * i + (t + 1))
                pool.sem_inc(s["apart_pool"], 1)
                ch.did(nc.gpsimd.tensor_scalar(idf[:, t, 0], idx[:, t, 0], float(NK), 0.0, ALU.mult, ALU.add))
                ch.did(nc.gpsimd.tensor_copy(idf[:, t, 1], idx[:, t, 1]))
                ch.wait()
                for a0, na_, nb_, at in SPANS:
                    ch.did(nc.gpsimd.tensor_tensor(
                        cexp[:, at:at + na_ * nb_, t, :].rearrange("p (a b) h -> p a b h", b=nb_),
                        idf[:, t, 0, :, a0:a0 + na_].rearrange("p h (a o) -> p a o h", o=1).to_broadcast([128, na_, nb_, NH]),
                        idf[:, t, 1, :, 0:nb_].rearrange("p h (o b) -> p o b h", o=1).to_broadcast([128, na_, nb_, NH]), ALU.add))
                ch.wait()
                pool.wait_ge(s["hit_ready"], 2 * i + (t + 1))
                h4 = hit[:, :, t, :].rearrange("p c (h k) -> p c h k", h=NH)
                nc.gpsimd.tensor_tensor(h4, h4, cexp[:, :, t, :].rearrange("p c (h o) -> p c h o", o=1).to_broadcast([128, NCAND, NH, TOPK]),
                                        ALU.mult).then_inc(s["expert_ready"], 1)

            def residual(i):
                for t in range(2):
                    last = nc.gpsimd.tensor_copy(x2s[:, t, :], x2T[:, bass.ds(i * 2 * TILE + t * TILE, TILE)])
                last.then_inc(s["x2s_ready"], 1)
            def mix(i):
                pool.wait_ge(s["mix_copied"], i + 1)
                pool.wait_ge(s["h_done"], (V // 2) * (i + 1))
                pool.sem_inc(s["apart_pool"], 1)
                for t in range(2):
                    nc.gpsimd.tensor_tensor(act_w[:, t], act_w[:, t], gelu[:, :, bass.ds(i * 2 * TILE + t * TILE, TILE)], ALU.mult).then_inc(s["mixed"], 1)

            pool.wait_ge(s["t_copied"], 8)
            residual(0)
            experts(0, 0)
            experts(0, 1)
            experts(1, 0)
            experts(1, 1)

            def duo(i, ahead=True):
                mix(i - 1)
                if ahead:
                    experts(i + 1, 0)
                pool.wait_ge(s["out_psum"], i)
                pool.sem_inc(s["apart_pool"], 1)
                residual(i)
                if ahead:
                    experts(i + 1, 1)
            with pool.Fori(0, (DUOS - 3) // 2) as i:
                ch.enter(i, 24)
                for j in range(2):
                    duo(2 * i + (1 + j))
            ch.leave((DUOS - 3) // 2)
            duo(DUOS - 2)
            duo(DUOS - 1, False)

        def within(p):
            return not isinstance(p, int) or 0 <= p < PAIRS

        def after(p, n):
            return not isinstance(p, int) or p >= n

        def before(i, n):
            return not isinstance(i, int) or i + n < DUOS

        def at(p, n):
            return isinstance(p, int) and p == n

        def self_attention(eng, step, chain=None, per_pass=0):
            for p in range(-AHEAD, AHEAD):
                step(p, p % 2)
            with eng.Fori(0, LOOPED // 2) as i:
                if chain:
                    chain.enter(i, per_pass)
                for j in range(2):
                    step(2 * i + (AHEAD + j), (AHEAD + j) % 2)
            if chain:
                chain.leave(LOOPED // 2)
            for p in range(AHEAD + LOOPED, PAIRS + 2):
                step(p, p % 2)

        @block.scalar
        def _(act):
            def ctx_copies(p, par, groups=range(NG), banks=T_BANKS):
                for g in groups:
                    act.wait_ge(s["cT_psum1"], NG * p + (g + 1))
                    nc.scalar.activation(ctxT[par][:, 1, g, :], bank(banks[g][1], 0, TG * ROWS), ACT.Copy).then_inc(s["cT_a"], 1)

            def table_ahead(n, function):
                nc.scalar.activation(spare[:, n:n + 1], ident[:, 0:1], function)

            def first_deviations(n):
                half = slice(n * PAIRS // 2, (n + 1) * PAIRS // 2)
                act.wait_ge(s["ln1_var"], n + 1)
                nc.scalar.activation(rstd[:, half], veps[:, half], ACT.Sqrt).then_inc(s["ln1_std"], 1)
            first_deviations(0)
            act.sem_inc(s["res_ready"], 1)
            act.wait_ge(s["zeros_done"], 1)

            def softmax(p, par):
                act.wait_ge(s["s1_read"], p + 1)
                nc.scalar.activation(prob1[par][:, :, 0:T], prob1[par][:, :, 0:T], ACT.Exp, scale=HD ** -0.5).then_inc(s["p1_ready"], 1)

            def att_copy(p):
                act.wait_ge(s["attT_psum"], p + 1)
                nc.scalar.activation(attT, bank(7, 0, 128), ACT.Copy).then_inc(s["attT_ready"], 1)

            def values(p, par):
                act.wait_ge(s["v_psum"], p + 1)
                if after(p, 2):
                    act.wait_ge(s["o1_psum"], p - 1)
                for a in range(2):
                    r = slice(a * TP, (a + 1) * TP)
                    nc.scalar.activation(vx[par][r, :, :, a * HD:(a + 1) * HD], bank(5, 0, 128)[r].rearrange("p (b h d) -> p b h d", b=2, d=HD),
                                         ACT.Copy).then_inc(s["vx_ready"], 1)

            def row_copy(p, par):
                act.wait_ge(s["xcT_psum"], p + 1)
                nc.scalar.activation(xcT[par], bank(6, 256, 384), ACT.Copy).then_inc(s["xcT_ready"], 1)

            def prob_copy(p):
                for g in range(2):
                    act.wait_ge(s["p1T_psum"], 2 * p + (g + 1))
                    nc.scalar.activation(prob1T[:, 4 * g:4 * g + 4, :], bank(3 + g).rearrange("p (h n) -> p h n", h=4), ACT.Copy).then_inc(s["p1T_ready"], 1)

            def step(p, par):
                if within(p - 1):
                    softmax(p - 1, 1 - par)
                if at(p, PAIRS - 1):
                    deviations(0, PAIRS - 4, 1)
                    act.wait_ge(s["folded"], 2)
                    for n, dst in enumerate((A2, Wvp)):
                        nc.scalar.activation(dst[:, :], bank(0, n * 128, n * 128 + 128), ACT.Copy).then_inc(s["fold_copied"], 1)
                if at(p, PAIRS):
                    ctx_copies(0, 0, (0,), T_BANKS_0)
                if within(p - 2):
                    att_copy(p - 2)
                if at(p, PAIRS):
                    rows_copy(0)
                if at(p, PAIRS + 1):
                    ctx_copies(0, 0, (1,), T_BANKS_0)
                    rows_copy(1)
                if within(p):
                    values(p, par)
                if within(p + 2):
                    row_copy(p + 2, par)
                if at(p, 1):
                    first_deviations(1)
                if within(p - 1):
                    prob_copy(p - 1)
                if at(p, PAIRS):
                    queries_copy(0)

            def deviations(p0, p1, n):
                act.wait_ge(s["ln_var"], n)
                nc.scalar.activation(rstd[:, p0:p1], veps[:, p0:p1], ACT.Sqrt).then_inc(s["ln_std"], 1)

            def rows_copy(g):
                act.wait_ge(s["t_psum"], g + 1)
                nc.scalar.activation(xl2T[:, g * BANK:(g + 1) * BANK], bank(X_BANK), ACT.Copy).then_inc(s["t_copied"], 1)

            def queries_copy(g):
                act.wait_ge(s["q2_psum"], g + 1)
                nc.scalar.activation(q2T[:, g * BANK:(g + 1) * BANK], bank(Q_BANKS[g]), ACT.Copy).then_inc(s["q2_copied"], 1)

            self_attention(act, step)

            def prob_copies(p):
                for g in (0, 2):
                    act.wait_ge(s["p2T_psum"], NG * p + (g + 1))
                    nc.scalar.activation(prob2T[0:ROWS, g * TG:(g + 1) * TG, :],
                                         bank(P_BANKS[g])[0:ROWS, :].rearrange("p (t n) -> p t n", t=TG),
                                         ACT.Copy).then_inc(s["p2T_a"], 1)

            def exps(p, par):
                act.wait_ge(s["m2_ready"], p + 1)
                nc.scalar.activation(prob2[par].rearrange("p (g m) -> p g m", g=NG), PS[:, 0:NG, 0:TG * ROWS], ACT.Exp,
                                     bias=nb2[:, 0:1], scale=0.25, accum_out=sum2[:, par:par + 1]).then_inc(s["p2_ready"], 1)

            def out_copy(p):
                act.wait_ge(s["o2T_psum"], p + 1)
                nc.scalar.activation(oT, bank(7, 128, 256), ACT.Copy).then_inc(s["oT_ready"], 1)

            queries_copy(1)
            ctx_copies(0, 0, (2,), T_BANKS_0)
            rows_copy(2)
            deviations(PAIRS - 4, PAIRS, 2)
            queries_copy(2)
            table_ahead(1, ACT.Exp)
            rows_copy(3)
            ctx_copies(1, 1, (0,))
            queries_copy(3)
            exps(0, 0)
            ctx_copies(1, 1, (1, 2))
            prob_copies(0)
            exps(1, 1)

            def step(p, par):
                out_copy(p - 1)
                ctx_copies(p + 1, 1 - par)
                prob_copies(p)
                exps(p + 1, 1 - par)
            with act.Fori(0, 3) as i:
                for j in range(4):
                    step(4 * i + (j + 1), (j + 1) % 2)
            step(13, 1)
            deviations(0, PAIRS - 4, 3)
            step(14, 0)
            out_copy(14)
            table_ahead(0, ACT.Sqrt)
            prob_copies(15)

            def token_copies(n0, n1):
                for n in range(n0, n1):
                    normal, g, b = TURNS[n]
                    act.wait_ge(s["t_psum"], 4 + n + 1)
                    nc.scalar.activation((xlT if normal else x2T)[:, g * 448:(g + 1) * 448].rearrange("p (a t) -> p a t", t=T),
                                         bank(b).rearrange("p (a t) -> p a t", t=TP)[:, :, 0:T], ACT.Copy).then_inc(s["t_copied"], 1)
            token_copies(0, 2)
            out_copy(15)
            token_copies(2, 6)
            deviations(PAIRS - 4, PAIRS, 4)
            token_copies(6, 7)
            act.wait_ge(s["bn_var"], 1)
            nc.scalar.activation(bsc[:, 1:2], bsc[:, 0:1], ACT.Sqrt).then_inc(s["bn_std"], 1)
            act.wait_ge(s["folded"], 3)
            nc.scalar.activation(Wsim[:, :], bank(7), ACT.Copy).then_inc(s["fold_copied"], 1)
            token_copies(7, 8)
            act.wait_ge(s["bn_ready"], 1)

            def normed(i, t):
                act.wait_ge(s["sim_psum"], 2 * i + (t + 1))
                nc.scalar.activation(xbn[:, t, :], xlT[:, bass.ds(i * 2 * TILE + t * TILE, TILE)], ACT.Identity,
                                     scale=bsc[:, 2:3], bias=bsc[:, 3:4]).then_inc(s["xbn_ready"], 1)

            def weights(i, t):
                act.wait_ge(s["best_ready"], 2 * i + (t + 1))
                if after(i, 1) and t == 0:
                    act.wait_ge(s["ew_psum"], i)
                nc.scalar.activation(weight[:, t, :].rearrange("p (h k) -> p h k", h=NH), best[:, t], ACT.Sigmoid).then_inc(s["weight_ready"], 1)

            def mix_copies(i):
                act.wait_ge(s["mix_psum"], i + 2)
                for b in range(4):
                    last = nc.scalar.activation(act_w[:, :, :, b * 32:(b + 1) * 32].rearrange("p t v n -> p (t v) n"),
                                                bank(b).rearrange("p (n w) -> p w n", w=2 * V), ACT.Copy, scale=1.0 / W_UP)
                last.then_inc(s["mix_copied"], 1)

            def rows(i):
                act.wait_ge(s["out_psum"], i + 1)
                act.wait_ge(s["out_done"], 16 * i + 16)
                nc.scalar.activation(res[:, :, :], bank(7, 0, 256).rearrange("p (t c) -> p t c", t=2), ACT.Copy).then_inc(s["res_ready"], 1)

            def gelus(i):
                for r in range(V // 2):
                    act.wait_ge(s["h_psum"], (V // 2) * i + (r + 1))
                    nc.scalar.activation(gelu[:, 2 * r:2 * r + 2, bass.ds(i * 2 * TILE, 2 * TILE)],
                                         bank(6 + r % 2).rearrange("p (v n) -> p v n", v=2), ACT.Gelu).then_inc(s["h_done"], 1)

            def expert_copies(i):
                act.wait_ge(s["ew_psum"], i + 1)
                nc.scalar.activation(eT[:, :], bank(6, 0, 128), ACT.Copy)
                nc.scalar.activation(w_hi[:, :], bank(6, 128, 256), ACT.Copy, scale=W_UP).then_inc(s["ew_copied"], 1)

            def first_u(i):
                act.wait_ge(s["eu8_ready"], i + 1)
                nc.scalar.activation(pick_u[:, 0:V, :], eu8[:, :, :], ACT.Relu, scale=-1.0, bias=1.0).then_inc(s["first_u"], 1)

            def duo(i):
                if after(i, 1):
                    mix_copies(i - 1)
                if before(i, 2):
                    normed(i + 2, 0)
                expert_copies(i)
                if before(i, 1):
                    weights(i + 1, 0)
                if after(i, 1):
                    rows(i - 1)
                first_u(i)
                gelus(i)
                if before(i, 2):
                    normed(i + 2, 1)
                if before(i, 1):
                    weights(i + 1, 1)
            for n in range(2):
                for t in range(2):
                    normed(n, t)
            for t in range(2):
                weights(0, t)
            duo(0)
            with act.Fori(0, (DUOS - 3) // 2) as i:
                for j in range(2):
                    duo(2 * i + (1 + j))
            duo(DUOS - 2)
            duo(DUOS - 1)
            rows(DUOS - 1)

        @block.vector
        def _(dve):
            ch = Chain(dve, s["dve"])

            def aggregates(p0, p1):
                ch.wait()
                for p in range(p0, p1):
                    ch.did(nc.vector.bn_aggr(mv[:, p, :], stats[:, p, :]))

            def variances(done, p0=0, p1=PAIRS):
                ch.wait()
                nc.vector.tensor_scalar_add(veps[:, p0:p1], mv[:, p0:p1, 1], LN_EPS).then_inc(s[done], 1)

            def pair_stats(src, p):
                ch.did(nc.vector.bn_stats(stats[:, bass.ds(p, 1), :].rearrange("p o c -> p (o c)"), src[:, bass.ds(p, 1), :].rearrange("p o c -> p (o c)")))

            def inverse(p0, p1):
                ch.did(nc.vector.reciprocal(rstd[:, p0:p1], rstd[:, p0:p1]))
                ch.wait()

            def layer_norm(src, p0, p1):
                for p in range(p0, p1):
                    last = nc.vector.tensor_scalar(xn_[:, p, :], src[:, p, :], mv[:, p, 0:1], rstd[:, p:p + 1], ALU.subtract, ALU.mult)
                    if p % 4 == 3 or p == p1 - 1:
                        last.then_inc(s["ln_done"], 1)
                    else:
                        last.then_inc(s["dve"], 1)
                        ch.n += 1

            def ctx_copies(p, par, groups=range(NG), banks=T_BANKS):
                for g in groups:
                    dve.wait_ge(s["cT_psum0"], NG * p + (g + 1))
                    nc.vector.tensor_copy(ctxT[par][:, 0, g, :], bank(banks[g][0], 0, TG * ROWS)).then_inc(s["cT_d"], 1)

            dve.wait_ge(s["pads_in"], 32)

            def first_norm(n):
                a, z = n * PAIRS // 2, (n + 1) * PAIRS // 2
                dve.wait_ge(s[f"x_in{n}"], 32)
                for p in range(a, z):
                    ch.did(nc.vector.bn_stats(stats[:, p, :], x0[:, p, :]))
                aggregates(a, z)
                variances("ln1_var", a, z)

            def first_inverse(n):
                dve.wait_ge(s["ln1_std"], n + 1)
                inverse(n * PAIRS // 2, (n + 1) * PAIRS // 2)
            first_norm(0)
            first_inverse(0)
            dve.wait_ge(s["ka_in"], 16)

            def normed(p, par):
                nc.vector.tensor_scalar(xc[par], x0[:, bass.ds(p, 1), :].rearrange("p o c -> p (o c)"), mv[:, bass.ds(p, 1), 0],
                                        rstd[:, bass.ds(p, 1)], ALU.subtract, ALU.mult).then_inc(s["xc_ready"], 1)

            def rotate(p, par):
                dve.wait_ge(s["qk_psum"], p + 1)
                if after(p, 1):
                    dve.wait_ge(s["rot_q_ready"], p)
                nc.vector.tensor_tensor(rope.rearrange("p (t r n) -> p t r n", t=2, r=2), bank(0).rearrange("p (t r n) -> p t r n", t=2, r=2),
                                        KA[:, ca["cos"][0]:ca["sin"][1]].rearrange("p (t o n) -> p t o n", t=2, o=1).to_broadcast([128, 2, 2, 128]),
                                        ALU.mult).then_inc(s["rope_ready"], 1)
                dve.wait_ge(s["rope_ready"], p + 1)
                if after(p, 1):
                    dve.wait_ge(s["kx_ready"], p)
                ch.did(nc.vector.tensor_tensor(rot_k, rope[:, 128:256], rope[:, 384:512], ALU.add))
                ch.wait()
                nc.vector.tensor_tensor(kx[par], rot_k.rearrange("p (o n) -> p o n", o=1).to_broadcast([128, 4, 128]),
                                        wa("slot").rearrange("p (g o) -> p g o", o=1).to_broadcast([128, 4, 128]), ALU.mult).then_inc(s["kx_ready"], 1)

            def softmax(p, par):
                dve.wait_ge(s["s1_psum"], p + 1)
                S = PS[:, 1:3, :].rearrange("p b (h k) -> p (b h) k", k=TP)[:, :, 0:T]
                ch.did(nc.vector.tensor_reduce(neg1[:, :], S, AX.X, ALU.max, negate=True))
                ch.wait()
                nc.vector.tensor_tensor(prob1[par][:, :, 0:T], S, neg1[:, :].rearrange("p (h o) -> p h o", o=1).to_broadcast([128, HEADS, T]),
                                        ALU.add).then_inc(s["s1_read"], 1)

            def normalise1(p):
                dve.wait_ge(s["o1_psum"], p + 1)
                o = bank(6, 0, HEADS // 2 * VW).rearrange("p (h d) -> p h d", d=VW)
                ch.did(nc.vector.reciprocal(inv1[:, :].rearrange("p (h a) -> p h a", a=2), o[:, :, 2 * HD:VW]))
                ch.wait()
                nc.vector.tensor_tensor(att.rearrange("p (h a d) -> p h a d", a=2, d=HD), o[:, :, 0:2 * HD].rearrange("p h (a d) -> p h a d", a=2),
                                        inv1[:, :].rearrange("p (h a o) -> p h a o", a=2, o=1).to_broadcast([128, HEADS // 2, 2, HD]),
                                        ALU.mult).then_inc(s["att_ready"], 1)

            def residual1(p):
                dve.wait_ge(s["y1_psum"], p + 1)
                dve.wait_ge(s["bias_added"], p + 1)
                nc.vector.tensor_tensor(x1[:, bass.ds(p, 1), :], bank(7, 128, 256).rearrange("p (o n) -> p o n", o=1),
                                        x1[:, bass.ds(p, 1), :], ALU.add).then_inc(s["x1_done"], 1)
                dve.wait_ge(s["x1_done"], p + 1)
                pair_stats(x1, p)

            def step(p, par):
                if within(p - 2):
                    normalise1(p - 2)
                if within(p + 1):
                    rotate(p + 1, 1 - par)
                if within(p + 3):
                    normed(p + 3, 1 - par)
                if within(p):
                    softmax(p, par)
                if at(p, 0):
                    first_norm(1)
                if at(p, AHEAD - 1):
                    first_inverse(1)
                if at(p, PAIRS - 2):
                    aggregates(0, PAIRS - 4)
                    variances("ln_var", 0, PAIRS - 4)
                if at(p, PAIRS - 1):
                    dve.wait_ge(s["ln_std"], 1)
                    inverse(0, PAIRS - 4)
                    layer_norm(x1, 0, 4)
                if at(p, PAIRS) or at(p, PAIRS + 1):
                    ctx_copies(0, 0, (p - PAIRS,), T_BANKS_0)
                if within(p - 2):
                    residual1(p - 2)
                if at(p, PAIRS):
                    layer_norm(x1, 4, 8)
            self_attention(dve, step, ch, 2 * 4)
            layer_norm(x1, 8, PAIRS - 4)
            aggregates(PAIRS - 4, PAIRS)
            variances("ln_var", PAIRS - 4, PAIRS)

            def maximum(p):
                dve.wait_ge(s["s2_psum"], p + 1)
                ch.did(nc.vector.tensor_reduce(max2[:, :], PS[:, 0:NG, 0:TG * ROWS], AX.XY, ALU.max))
                ch.wait()
                nc.vector.tensor_scalar_mul(nb2[:, :], max2[:, :], -0.25).then_inc(s["m2_ready"], 1)

            def prob_copy(p, par):
                dve.wait_ge(s["p2_ready"], p + 1)
                nc.vector.reciprocal(inv2[:, par:par + 1], sum2[:, par:par + 1]).then_inc(s["dve"], 1)
                ch.n += 1
                dve.wait_ge(s["p2T_psum"], NG * p + 2)
                nc.vector.tensor_copy(prob2T[0:ROWS, TG:2 * TG, :],
                                      bank(P_BANKS[1])[0:ROWS, :].rearrange("p (t n) -> p t n", t=TG)).then_inc(s["p2T_d"], 1)

            def residual(p, par):
                dve.wait_ge(s["y2_psum"], p + 1)
                nc.vector.tensor_tensor(x2[:, bass.ds(p, 1), :], bank(7, 256, 384).rearrange("p (o n) -> p o n", o=1),
                                        x1[:, bass.ds(p, 1), :], ALU.add).then_inc(s["x2_done"], 1)
                dve.wait_ge(s["x2_done"], p + 2)
                pair_stats(x2, p)

            def normalise(p, par):
                dve.wait_ge(s["o2_psum"], p + 1)
                nc.vector.tensor_scalar(o2, bank(7, 0, 128), inv2[:, par:par + 1], None, ALU.mult).then_inc(s["o2_ready"], 1)

            ctx_copies(0, 0, (2,), T_BANKS_0)
            dve.wait_ge(s["ln_std"], 2)
            inverse(PAIRS - 4, PAIRS)
            layer_norm(x1, PAIRS - 4, PAIRS)
            dve.wait_ge(s["ln_done"], 4)
            ch.did(nc.vector.tensor_tensor(x1, x1, wa("bias2").rearrange("p (o c) -> p o c", o=1).to_broadcast([128, PAIRS, C]), ALU.add))
            ch.wait()
            dve.sem_inc(s["x2_done"], 1)
            maximum(0)
            ctx_copies(1, 1)
            prob_copy(0, 0)
            maximum(1)

            def step(p, par):
                normalise(p - 1, 1 - par)
                ctx_copies(p + 1, 1 - par)
                residual(p - 1, 1 - par)
                prob_copy(p, par)
                maximum(p + 1)
            with dve.Fori(0, 3) as i:
                ch.enter(i, 4 * 3)
                for j in range(4):
                    step(4 * i + (j + 1), (j + 1) % 2)
            ch.leave(3)
            step(13, 1)
            aggregates(0, PAIRS - 4)
            variances("ln_var", 0, PAIRS - 4)
            step(14, 0)
            dve.wait_ge(s["ln_std"], 3)
            inverse(0, PAIRS - 4)
            normalise(14, 0)
            layer_norm(x2, 0, 8)
            residual(14, 0)
            prob_copy(15, 1)
            layer_norm(x2, 8, PAIRS - 4)
            normalise(15, 1)

            def token_stats(g):
                dve.wait_ge(s["t_copied"], 4 + TURNS.index((1, g, g)) + 1)
                ch.did(nc.vector.bn_stats(bst[:, g, :], xlT[:, g * 448:(g + 1) * 448]))
            for g in range(2):
                token_stats(g)
            residual(15, 1)
            aggregates(PAIRS - 4, PAIRS)
            variances("ln_var", PAIRS - 4, PAIRS)
            token_stats(2)
            dve.wait_ge(s["ln_std"], 4)
            inverse(PAIRS - 4, PAIRS)
            layer_norm(x2, PAIRS - 4, PAIRS)
            token_stats(3)
            ch.wait()
            ch.did(nc.vector.bn_aggr(bmv[:, :], bst[:, :, :].rearrange("p a b -> p (a b)")))
            ch.wait()
            nc.vector.tensor_scalar_add(bsc[:, 0:1], bmv[:, 1:2], BN_EPS).then_inc(s["bn_var"], 1)
            dve.wait_ge(s["bn_std"], 1)
            ch.did(nc.vector.reciprocal(bsc[:, 0:1], bsc[:, 1:2]))
            ch.wait()
            ch.did(nc.vector.tensor_tensor(bsc[:, 2:3], bsc[:, 0:1], wa("gamma"), ALU.mult))
            ch.wait()
            ch.did(nc.vector.tensor_tensor(bsc[:, 0:1], bmv[:, 0:1], bsc[:, 2:3], ALU.mult))
            ch.wait()
            nc.vector.tensor_tensor(bsc[:, 3:4], wa("beta"), bsc[:, 0:1], ALU.subtract).then_inc(s["bn_ready"], 1)
            dve.sem_inc(s["sim_read"], 2)

            def best_keys(i, t):
                dve.wait_ge(s["sim_psum"], 2 * i + (2 + t + 1))
                if after(i, 1):
                    dve.wait_ge(s["expert_ready"], 2 * i + (t - 1))
                    dve.wait_ge(s["weight_ready"], 2 * i + (t - 1))
                dve.sem_inc(s["apart"], 1)
                v_t, i_t = val[:, t], idx[:, t]
                sim = bank(4 + t).rearrange("p (a h k) -> p a h k", a=2, h=NH)

                def places(a):
                    for h in range(NH):
                        ch.did(nc.vector.max_index(i_t[:, a, h, :], v_t[:, a, h, :], sim[:, a, h, :]))

                for a in range(2):
                    for h in range(NH):
                        ch.did(nc.vector.max(v_t[:, a, h, :], sim[:, a, h, :]))
                ch.wait_apart(s["apart"], but=NH)
                places(0)
                ch.wait(but=NH)
                for a0, na_, nb_, at in SPANS:
                    ch.did(nc.vector.tensor_tensor(
                        cand[:, t, :, at:at + na_ * nb_].rearrange("p h (a b) -> p h a b", b=nb_),
                        v_t[:, 0, :, a0:a0 + na_].rearrange("p h (a o) -> p h a o", o=1).to_broadcast([128, NH, na_, nb_]),
                        v_t[:, 1, :, 0:nb_].rearrange("p h (o b) -> p h o b", o=1).to_broadcast([128, NH, na_, nb_]), ALU.add))
                places(1)
                ch.wait_apart(s["apart"], but=NH)
                for h in range(NH):
                    ch.did(nc.vector.max(best[:, t, h, :], cand[:, t, h, :]))
                ch.wait(but=NH)
                dve.sem_inc(s["sim_read"], 1)
                dve.sem_inc(s["index_ready"], 1)
                ch.wait_apart(s["apart"])
                dve.sem_inc(s["best_ready"], 1)
                for h in range(NH):
                    ch.did(nc.vector.max_index(pos[:, t, h, :], best[:, t, h, :], cand[:, t, h, :]))

            def mark(i, t, but=0):
                ch.wait(but)
                if after(i, 1):
                    dve.wait_ge(s["ew_psum"], i)
                nc.vector.tensor_tensor(
                    hit[:, :, t, :], pos[:, t].rearrange("p (o h) k -> p o (h k)", o=1).to_broadcast([128, NCAND, HK]),
                    iota_c[:, :, :], ALU.is_equal).then_inc(s["hit_ready"], 1)

            def parts(i):
                dve.wait_ge(s["ew_copied"], i + 1)
                ch.did(nc.vector.scalar_tensor_tensor(w_lo[:, :], bank(6, 128, 256), W_UP, w_hi[:, :], ALU.mult, ALU.subtract))
                ch.did(nc.vector.tensor_single_scalar(ev[:, :], eT[:, :], V - 1, op=ALU.bitwise_and))
                ch.did(nc.vector.tensor_single_scalar(eu[:, :], eT[:, :], V.bit_length() - 1, op=ALU.logical_shift_right))

            def picks(i):
                dve.wait_ge(s["mix_psum"], i + 1)
                ch.wait()
                dve.sem_inc(s["ew_read"], 1)
                ch.did(nc.vector.tensor_tensor(pick_v[:, :, :], ev[:, :].rearrange("p (o n) -> p o n", o=1).to_broadcast([128, V, TILE]),
                                               iota_v[:, :, :], ALU.is_equal))
                ch.did(nc.vector.tensor_tensor(eu8[:, :, :], eu[:, :].rearrange("p (o n) -> p o n", o=1).to_broadcast([128, V, TILE]),
                                               iota_v[:, :, :], ALU.bitwise_xor))
                ch.wait()
                dve.sem_inc(s["eu8_ready"], 1)
                for t in range(2):
                    for dst, w in ((b_hi, w_hi), (b_lo, w_lo)):
                        r = slice(t * HK, (t + 1) * HK)
                        ch.did(nc.vector.tensor_tensor(dst[r, t * V:(t + 1) * V, :], pick_v[r, :, :],
                                                       w[r, :].rearrange("p (o n) -> p o n", o=1).to_broadcast([HK, V, TILE]), ALU.mult))
                for a in range(1, U // V):
                    ch.did(nc.vector.tensor_single_scalar(pick_u[:, a * V:(a + 1) * V, :], eu8[:, :, :], a * V, op=ALU.is_equal))
                ch.wait()
                dve.sem_inc(s["picks"], 1)

            dve.wait_ge(s["iota_done"], 1)

            for t in range(2):
                best_keys(0, t)
                mark(0, t)

            def duo(i):
                best_keys(i + 1, 0)
                parts(i)
                mark(i + 1, 0, but=3)
                picks(i)
                best_keys(i + 1, 1)
                mark(i + 1, 1)
            with dve.Fori(0, (DUOS - 1) // 2) as i:
                ch.enter(i, 2 * (2 * (16 + 16 + 4 + 8 + 8) + 3 + 2 + 4 + U // V - 1))
                for j in range(2):
                    duo(2 * i + j)
            ch.leave((DUOS - 1) // 2)
            parts(DUOS - 1)
            picks(DUOS - 1)
            dve.wait_ge(s["h_done"], (V // 2) * DUOS)
            for b in range(4):
                dve.wait_ge(s["bank_spread"], b + 1)
                for t in range(2):
                    n0 = (DUOS - 1) * 2 * TILE + t * TILE + b * 32
                    last = nc.vector.scalar_tensor_tensor(
                        act_w[:, t, :, b * 32:(b + 1) * 32], bank(b).rearrange("p (n t v) -> p t v n", t=2, v=V)[:, t], 1.0 / W_UP,
                        gelu[:, :, n0:n0 + 32], ALU.mult, ALU.mult)
                    last.then_inc(s["mixed" if b == 3 else "dve"], 1)
                    ch.n += b < 3
                if b == 2:
                    ch.wait()

        @block.tensor
        def _(pe):
            mm = nc.tensor.matmul
            one = dict(start=True, stop=True)
            pe.wait_ge(s["ka_in"], 16)

            def projections(p, par):
                pe.wait_ge(s["xcT_ready"], p + 1)
                if after(p, 1):
                    pe.wait_ge(s["rope_ready"], p)
                for n, w in enumerate(("wq", "wk", "wqs", "wks")):
                    last = mm(bank(0, n * 128, n * 128 + 128), wa(w), xcT[par], **one)
                last.then_inc(s["qk_psum"], 1)

            def turn1(p):
                pe.wait_ge(s["att_ready"], p + 1)
                if after(p, 1):
                    pe.wait_ge(s["x1_done"], p)
                nc.tensor.transpose(bank(7, 0, 128), att, ident).then_inc(s["attT_psum"], 1)

            def values(p, par):
                if after(p, 1):
                    pe.wait_ge(s["vx_ready"], 2 * p)
                for b in range(2):
                    for a in range(2):
                        last = mm(bank(5, b * 64, b * 64 + 64)[a * TP:(a + 1) * TP, :], xcT[par][:, b * TP:(b + 1) * TP],
                                  wa("wv")[:, a * 64:a * 64 + 64], **one)
                last.then_inc(s["v_psum"], 1)

            def turn_rows(p, par):
                pe.wait_ge(s["xc_ready"], p + 1)
                if after(p, 5):
                    pe.wait_ge(s["att_ready"], p - 3)
                nc.tensor.transpose(bank(6, 256, 384), xc[par], ident).then_inc(s["xcT_psum"], 1)

            def scores1(p, par, half):
                if half == 0:
                    pe.wait_ge(s["qx_ready"], p + 1)
                    pe.wait_ge(s["kx_ready"], p + 1)
                    if after(p, 1):
                        pe.wait_ge(s["s1_read"], p)
                for g in (2 * half, 2 * half + 1):
                    for b in range(2):
                        o = PS[b * TP:(b + 1) * TP, 1 + g // 2, (g % 2) * 256:(g % 2) * 256 + 256].rearrange("p (h k) -> p h k", k=TP)[:, :, 0:T]
                        last = mm(o, qx[par][:, g, b * TP:(b + 1) * TP], kx[par][:, :, b * TP:b * TP + T], **one)
                if half:
                    last.then_inc(s["s1_psum"], 1)

            def project1(p):
                pe.wait_ge(s["attT_ready"], p + 1)
                mm(bank(7, 128, 256), attT, wa("wproj"), **one).then_inc(s["y1_psum"], 1)

            def prob_transposes(p, par):
                pe.wait_ge(s["p1_ready"], p + 1)
                for h in range(HEADS // 2):
                    last = nc.tensor.transpose(bank(3 + h // 4, (h % 4) * 128, (h % 4) * 128 + 128),
                                               prob1[par][:, 2 * h:2 * h + 2, :].rearrange("p h k -> p (h k)"), ident)
                    if h % 4 == 3:
                        last.then_inc(s["p1T_psum"], 1)

            def products1(p, par):
                pe.wait_ge(s["xcT_ready"], min(p + 4, PAIRS) if isinstance(p, int) else p + 4)
                pe.wait_ge(s["vx_ready"], 2 * p + 2)
                for h in range(HEADS // 2):
                    if h % 4 == 0:
                        pe.wait_ge(s["p1T_ready"], 2 * p + (1 + h // 4))
                    for b in range(2):
                        last = mm(bank(6, h * VW, (h + 1) * VW)[b * TP:(b + 1) * TP, :],
                                  prob1T[:, h, b * TP:(b + 1) * TP], vx[par][:, b, h, :], **one)
                last.then_inc(s["o1_psum"], 1)

            def arrived(slot, use):
                pe.wait_ge(s[f"ctx{slot}"], 32 * use)

            def fold_projections():
                pe.wait_ge(s["rope_ready"], PAIRS)
                mm(bank(0, 0, 128), wa("xwq"), wa("xwk"), **one).then_inc(s["folded"], 1)
                mm(bank(0, 128, 256), wa("xwv"), wa("xproj"), **one).then_inc(s["folded"], 1)

            def fold_keys(n0, n1):
                pe.wait_ge(s["kb_in"], 32)
                for n in range(n0, n1):
                    last = mm(bank(7, n * NK, (n + 1) * NK), fwq[:, n * C:(n + 1) * C], wb("keys")[:, n * NK:(n + 1) * NK], **one)
                if n1 == 2 * NH:
                    last.then_inc(s["folded"], 1)

            def ctx_transposes(p, slot, groups=range(NG), banks=T_BANKS):
                for g in groups:
                    for b in range(2):
                        if banks is T_BANKS_0:
                            if g:
                                pe.wait_ge(s["cT_d" if b == 0 else "cT_a"], g)
                        elif g == 2:
                            pe.wait_ge(s["cT_d" if b == 0 else "cT_a"], NG * p + 1)
                        for k in range(TG):
                            last = nc.tensor.transpose(bank(banks[g][b], k * ROWS, (k + 1) * ROWS), ring[slot][0:ROWS, b, g * TG + k, :],
                                                       ident[0:ROWS, 0:ROWS])
                        last.then_inc(s[f"cT_psum{b}"], 1)

            def turn_four(g):
                pe.wait_ge(s["ln_done"], g + 1)
                if g == 0:
                    pe.wait_ge(s["vx_ready"], 2 * PAIRS)
                else:
                    pe.wait_ge(s["t_copied"], g)
                for a in range(4):
                    last = nc.tensor.transpose(bank(X_BANK, a * 128, a * 128 + 128), xn_[:, 4 * g + a, :], ident)
                last.then_inc(s["t_psum"], 1)

            def queries(g):
                pe.wait_ge(s["t_copied"], g + 1)
                if g == 0:
                    pe.wait_ge(s["fold_copied"], 2)
                elif g < 3:
                    pe.wait_ge(s["q2_copied"], g)
                else:
                    pe.wait_ge(s["x1_done"], PAIRS)
                mm(bank(Q_BANKS[g]), A2[:, :], xl2T[:, g * BANK:(g + 1) * BANK], **one).then_inc(s["q2_psum"], 1)

            def step(p, par):
                if at(p, PAIRS - 1):
                    fold_projections()
                if at(p, PAIRS):
                    arrived(0, 1)
                    pe.wait_ge(s["s1_read"], PAIRS)
                    ctx_transposes(0, 0, (0,), T_BANKS_0)
                if within(p + 1):
                    projections(p + 1, 1 - par)
                if within(p):
                    scores1(p, par, 0)
                if within(p - 2):
                    turn1(p - 2)
                if within(p + 2):
                    turn_rows(p + 2, par)
                if within(p):
                    scores1(p, par, 1)
                if at(p, PAIRS):
                    turn_four(0)
                if at(p, PAIRS + 1):
                    ctx_transposes(0, 0, (1,), T_BANKS_0)
                    turn_four(1)
                if within(p - 2):
                    project1(p - 2)
                if within(p - 1):
                    prob_transposes(p - 1, 1 - par)
                if within(p + 1):
                    values(p + 1, 1 - par)
                if within(p - 1):
                    products1(p - 1, 1 - par)
                if at(p, PAIRS):
                    queries(0)
            self_attention(pe, step)

            def scores(p, par):
                pe.wait_ge(s["q2_ready"], p + 1)
                for g in range(NG):
                    pe.wait_ge(s["cT_d"], NG * p + (g + 1))
                    pe.wait_ge(s["cT_a"], NG * p + (g + 1))
                    for b in range(2):
                        last = mm(PS[b * TP:(b + 1) * TP, g, 0:TG * ROWS], q2[par][:, b * TP:(b + 1) * TP], ctxT[par][:, b, g, :], **one)
                last.then_inc(s["s2_psum"], 1)

            def products(p, par, slot):
                pe.wait_ge(s["p2_ready"], p + 1)
                for g in range(NG):
                    for k in range(TG):
                        t = g * TG + k
                        last = nc.tensor.transpose(bank(P_BANKS[g], k * 128, k * 128 + 128)[0:ROWS, :],
                                                   prob2[par][:, t * ROWS:(t + 1) * ROWS], ident)
                    last.then_inc(s["p2T_psum"], 1)
                for g in range(NG):
                    if g == 1:
                        pe.wait_ge(s["p2T_d"], p + 1)
                    else:
                        pe.wait_ge(s["p2T_a"], 2 * p + (1 if g == 0 else 2))
                    for t in range(g * TG, (g + 1) * TG):
                        for b in range(2):
                            last = mm(bank(7, 0, 128)[b * TP:(b + 1) * TP, :], prob2T[0:ROWS, t, b * TP:(b + 1) * TP],
                                      ring[slot][0:ROWS, b, t, :], start=t == 0, stop=t == NT - 1)
                last.then_inc(s["o2_psum"], 1)

            def turn(p):
                pe.wait_ge(s["o2_ready"], p + 1)
                nc.tensor.transpose(bank(7, 128, 256), o2, ident).then_inc(s["o2T_psum"], 1)

            def project(p):
                pe.wait_ge(s["oT_ready"], p + 1)
                mm(bank(7, 256, 384), oT, Wvp[:, :], **one).then_inc(s["y2_psum"], 1)

            queries(1)
            ctx_transposes(0, 0, (2,), T_BANKS_0)
            turn_four(2)
            queries(2)
            pe.wait_ge(s["q2_copied"], 3)
            pe.wait_ge(s["cT_d"], NG)
            pe.wait_ge(s["cT_a"], NG)
            scores(0, 0)
            turn_four(3)
            arrived(1, 1)
            ctx_transposes(1, 1, (0,))
            queries(3)
            ctx_transposes(1, 1, (1, 2))
            pe.wait_ge(s["p2_ready"], 1)
            scores(1, 1)
            pe.wait_ge(s["q2_copied"], 4)
            products(0, 0, 0)

            def step(p, par, slot, use):
                arrived((slot + 1) % RING, use)
                ctx_transposes(p + 1, (slot + 1) % RING, (0,))
                turn(p - 1)
                ctx_transposes(p + 1, (slot + 1) % RING, (1, 2))
                project(p - 1)
                scores(p + 1, 1 - par)
                pe.wait_ge(s["x2_done"], p + 1)
                products(p, par, slot)
            with pe.Fori(0, 3) as i:
                for j in range(4):
                    step(4 * i + (j + 1), (j + 1) % 2, (j + 1) % RING, i + (1 + (j + 2) // RING))
            step(13, 1, 1, 4)
            step(14, 0, 2, 4)
            turn(14)
            project(14)
            pe.wait_ge(s["x2_done"], PAIRS)
            products(15, 1, 3)

            def token_turns(n0, n1):
                for n in range(n0, n1):
                    normal, g, b = TURNS[n]
                    if normal:
                        pe.wait_ge(s["ln_done"], 4 + g + 1)
                    elif g == 3:
                        pe.wait_ge(s["x2_done"], PAIRS + 1)
                        pe.wait_ge(s["t_copied"], 4 + 1)
                    for a in range(4):
                        last = nc.tensor.transpose(bank(b, a * 128, a * 128 + 128), (xn_ if normal else x2)[:, 4 * g + a, :], ident)
                    last.then_inc(s["t_psum"], 1)
            token_turns(0, 2)
            turn(15)
            token_turns(2, 4)
            project(15)
            token_turns(4, 6)
            pe.wait_ge(s["x2_done"], PAIRS + 1)
            fold_keys(0, 8)
            token_turns(6, 7)
            fold_keys(8, 2 * NH)
            token_turns(7, 8)
            pe.wait_ge(s["fold_copied"], 3)
            pe.wait_ge(s["t_copied"], 12)
            pe.sem_inc(s["mix_psum"], 1)
            pe.sem_inc(s["sim_psum"], 2)

            def hidden(i):
                for r in range(V // 2):
                    if r == 0:
                        pe.wait_ge(s["ew_read"], i + 1)
                    elif r == 1:
                        pe.wait_ge(s["res_ready"], i + 1)
                    else:
                        pe.wait_ge(s["h_done"], (V // 2) * i + (r - 1))
                    for k in range(2):
                        v = 2 * r + k
                        last = mm(bank(6 + r % 2, k * 256, k * 256 + 256), wb("down")[:, v * U:(v + 1) * U],
                                  xlT[:, bass.ds(i * 2 * TILE, 2 * TILE)], **one)
                    last.then_inc(s["h_psum"], 1)

            def key_scores(i, t):
                pe.wait_ge(s["xbn_ready"], 2 * i + (t + 1))
                pe.wait_ge(s["sim_read"], 2 * i + (t + 1))
                mm(bank(4 + t), xbn[:, t, :], Wsim[:, :], **one).then_inc(s["sim_psum"], 1)

            def weight_transpose(i):
                pe.wait_ge(s["weight_ready"], 2 * i + 2)
                if after(i, 1):
                    pe.wait_ge(s["h_done"], (V // 2) * i - 1)
                nc.tensor.transpose(bank(6, 128, 256), weight[:, :, :].rearrange("p t k -> p (t k)"), ident)

            def expert_transposes(i):
                pe.wait_ge(s["expert_ready"], 2 * i + 2)
                for n in range(NCAND):
                    last = mm(bank(6, 0, 128), hit[:, n, :, :].rearrange("p t k -> p (t k)"), ident16[:, :], start=n == 0, stop=n == NCAND - 1)
                last.then_inc(s["ew_psum"], 1)

            def spread(i, by_bank=False):
                pe.wait_ge(s["picks"], i + 1)
                pe.wait_ge(s["first_u"], i + 1)
                if after(i, 1):
                    pe.wait_ge(s["mix_copied"], i)
                for n in range(TILE):
                    o = bank(n // 32, (n % 32) * 16, (n % 32) * 16 + 16)
                    mm(o, pick_u[:, :, n], b_hi[:, :, n], start=True, stop=False)
                    last = mm(o, pick_u[:, :, n], b_lo[:, :, n], start=False, stop=True)
                    if by_bank and n % 32 == 31:
                        last.then_inc(s["bank_spread"], 1)
                if not by_bank:
                    last.then_inc(s["mix_psum"], 1)

            def gather(i):
                pe.wait_ge(s["x2s_ready"], i + 1)
                pe.wait_ge(s["h_done"], (V // 2) * (i + 1))
                pe.wait_ge(s["res_ready"], i + 1)
                for t in range(2):
                    o = bank(7, t * 128, t * 128 + 128)
                    mm(o, x2s[:, t, :], ident, start=True, stop=False)
                    pe.wait_ge(s["mixed"], 2 * i + (t + 1))
                    for v in range(V):
                        last = mm(o, act_w[:, t, v, :], wb("up")[:, v * C:(v + 1) * C], start=False, stop=v == V - 1)
                last.then_inc(s["out_psum"], 1)

            def duo(i):
                weight_transpose(i)
                if before(i, 1):
                    key_scores(i + 1, 1)
                expert_transposes(i)
                if after(i, 1):
                    gather(i - 1)
                if before(i, 2):
                    key_scores(i + 2, 0)
                hidden(i)
                spread(i, by_bank=not before(i, 1))
            key_scores(0, 0)
            key_scores(0, 1)
            key_scores(1, 0)
            duo(0)
            with pe.Fori(0, (DUOS - 3) // 2) as i:
                for j in range(2):
                    duo(2 * i + (1 + j))
            duo(DUOS - 2)
            duo(DUOS - 1)
            gather(DUOS - 1)


def constants():
    import numpy as np
    p = np.arange(128)
    inv = (1.0 / 10000.0 ** (np.arange(0, HD, 2, dtype=np.float32) / np.float32(HD))).astype(np.float32)
    ang = np.arange(T, dtype=np.float32)[None, :] * inv[(p % HD) // 2][:, None]
    cos = np.zeros((128, 2, TP), np.float32)
    sin = np.zeros((128, 2, TP), np.float32)
    cos[:, :, :T] = np.cos(ang)[:, None, :]
    sin[:, :, :T] = np.where(p % 2 == 0, -1.0, 1.0)[:, None, None] * np.sin(ang)[:, None, :]
    four = np.arange(4)
    return {
        "ident": np.eye(128, dtype=np.float32),
        "cos": cos.reshape(128, 2 * TP).astype(np.float32), "sin": sin.reshape(128, 2 * TP).astype(np.float32),
        "slot": ((p // HD % 4)[:, None] == four).astype(np.float32),
        "group": ((p // 32)[:, None] == four).astype(np.float32),
    }


def kernel(**inputs):
    import numpy as np
    import concourse.bacc as bacc
    from concourse.bass_utils import run_bass_kernel_spmd

    a = {k: np.asarray(v) for k, v in inputs.items()}
    qkv = a["L0_attn_w_qkv"]
    swapped = qkv.reshape(3 * C // 2, 2, C)[:, ::-1].reshape(3 * C, C)
    row = lambda b: np.broadcast_to(b[None, :], (128, C))
    cols = {
        "wq": qkv[:C].T, "wqs": swapped[:C].T, "wk": qkv[C:2 * C].T, "wks": swapped[C:2 * C].T,
        "wv": qkv[2 * C:].reshape(HEADS // 2, 2, HD, C).transpose(1, 0, 2, 3).reshape(C, C).T,
        "wproj": a["L0_attn_w_proj"].T,
        "xwq": a["L0_xattn_wq"].T, "xwk": a["L0_xattn_wk"].T, "xwv": a["L0_xattn_wv"].T, "xproj": a["L0_xattn_w_proj"],
        "bias1": row(a["L0_attn_b_proj"]), "bias2": row(a["L0_xattn_b_proj"]),
        "gamma": a["L0_ffn_bn_gamma"][:, None], "beta": a["L0_ffn_bn_beta"][:, None],
        "keys": a["L0_ffn_keys_p"].transpose(3, 2, 0, 1).reshape(C, -1),
        "down": a["L0_ffn_down"][:EXPERTS].reshape(U, V, C).transpose(2, 1, 0).reshape(C, -1),
        "up": a["L0_ffn_up"][:EXPERTS].reshape(U, V * C),
        **constants(),
    }
    arrays = {
        "x": np.ascontiguousarray(a["x"]), "zeros": np.zeros((TP - T, PAIRS, C), np.float32), "ctx": np.ascontiguousarray(a["ctx_1024"]),
        "pack_a": np.ascontiguousarray(np.concatenate([cols[n] for n, _ in PACK_A], axis=1)),
        "pack_b": np.ascontiguousarray(np.concatenate([cols[n] for n, _ in PACK_B], axis=1)),
        "pack_q": np.ascontiguousarray(a["L0_ffn_w_q"].reshape(2 * NH, C, C).transpose(1, 0, 2).reshape(C, -1)),
    }
    nc = bacc.Bacc("TRN2", target_bir_lowering=False, num_devices=1)
    args = [nc.dram_tensor(n, v.shape, mybir.dt.from_np(v.dtype), kind="ExternalInput").ap() for n, v in arrays.items()]
    out = nc.dram_tensor("out", (B, T, C), F32, kind="ExternalOutput").ap()
    decoder_block(nc, *args, out)
    r = run_bass_kernel_spmd(nc, [arrays], core_ids=[0])
    return r.results[0]["out"]
```
